# Optimizing a Trainium2 kernel written in Bass

```python
import numpy as np
import jax
import jax.numpy as jnp

def _softmax(x, axis=-1):
    return jax.nn.softmax(x, axis=axis)

def _gelu(x):
    return jax.nn.gelu(x, approximate=True)

def _silu(x):
    return jax.nn.silu(x)

def _sigmoid(x):
    return jax.nn.sigmoid(x)

def _layernorm(x, axis=-1, eps=1e-05):
    m = jnp.mean(x, axis=axis, keepdims=True)
    v = jnp.var(x, axis=axis, keepdims=True)
    return (x - m) / jnp.sqrt(v + eps)

def _scatter_add(tgt, idx, src, axis=0):
    return tgt.at[idx].add(src)

def _segment_sum(src, seg, n):
    return jax.ops.segment_sum(src, seg, n)
kernel_name = 'mk_seq_preln_d1_jaxref_r4_61c83c'

def setup_inputs(seed: int=0):
    np.random.seed(seed)
    _w = jnp.asarray

    def _L0_attn_setup():
        import jax, jax.numpy as jnp
        import numpy as np
        D_MODEL = 256
        N_HEADS = 16
        D_HEAD = D_MODEL // N_HEADS
        B, T = (2, 512)
        EPS = 1e-05
        key = jax.random.key(seed)
        ks = jax.random.split(key, 5)
        s = 1.0 / np.sqrt(D_MODEL)
        return {'x': jax.random.normal(ks[0], (B, T, D_MODEL), dtype=jnp.float32), 'W_q': jax.random.normal(ks[1], (D_MODEL, D_MODEL), dtype=jnp.float32) * s, 'W_k': jax.random.normal(ks[2], (D_MODEL, D_MODEL), dtype=jnp.float32) * s, 'W_v': jax.random.normal(ks[3], (D_MODEL, D_MODEL), dtype=jnp.float32) * s, 'W_o': jax.random.normal(ks[4], (D_MODEL, D_MODEL), dtype=jnp.float32) * s, 'gn_weight': jnp.ones((D_MODEL,), dtype=jnp.float32), 'gn_bias': jnp.zeros((D_MODEL,), dtype=jnp.float32)}
    _L0_attn_in = _L0_attn_setup()

    def _L0_ffn_setup():
        import jax, jax.numpy as jnp
        import numpy as np
        E = 8
        TOPK = 2
        PRIME = 11
        HASH_OFF = 7919
        N_SHARED = 1
        key = jax.random.key(seed)
        ks = jax.random.split(key, 8)
        B, T, C, Hs, Hr = (4, 2048, 256, 512, 256)
        sc = lambda k, shape, fan: jax.random.normal(k, shape, jnp.float32) * fan ** (-0.5)
        return {'x': jax.random.normal(ks[0], (B, T, C), jnp.float32), 't_emb': jax.random.normal(ks[1], (B, C), jnp.float32), 'sw1': sc(ks[2], (C, Hs), C), 'sb1': jnp.zeros((Hs,), jnp.float32), 'sw3': sc(ks[3], (C, Hs), C), 'sb3': jnp.zeros((Hs,), jnp.float32), 'sw2': sc(ks[4], (Hs, C), Hs), 'sb2': jnp.zeros((C,), jnp.float32), 'w1': sc(ks[5], (E, C, Hr), C), 'b1': jnp.zeros((E, Hr), jnp.float32), 'w2': sc(ks[6], (E, Hr, C), Hr), 'b2': jnp.zeros((E, C), jnp.float32)}
    _L0_ffn_in = _L0_ffn_setup()
    _d = {'L0_attn_x': _L0_attn_in['x'], 'L0_attn_W_q': _L0_attn_in['W_q'], 'L0_attn_W_k': _L0_attn_in['W_k'], 'L0_attn_W_v': _L0_attn_in['W_v'], 'L0_attn_W_o': _L0_attn_in['W_o'], 'L0_attn_gn_weight': _L0_attn_in['gn_weight'], 'L0_attn_gn_bias': _L0_attn_in['gn_bias'], 'L0_ffn_t_emb': _L0_ffn_in['t_emb'], 'L0_ffn_sw1': _L0_ffn_in['sw1'], 'L0_ffn_sb1': _L0_ffn_in['sb1'], 'L0_ffn_sw3': _L0_ffn_in['sw3'], 'L0_ffn_sb3': _L0_ffn_in['sb3'], 'L0_ffn_sw2': _L0_ffn_in['sw2'], 'L0_ffn_sb2': _L0_ffn_in['sb2'], 'L0_ffn_w1': _L0_ffn_in['w1'], 'L0_ffn_b1': _L0_ffn_in['b1'], 'L0_ffn_w2': _L0_ffn_in['w2'], 'L0_ffn_b2': _L0_ffn_in['b2']}
    _x0 = _d['L0_attn_x']
    _d['L0_attn_x'] = jax.random.normal(jax.random.fold_in(jax.random.key(seed), 1), (4, 1024, 256), dtype=_x0.dtype)
    del _x0
    return _d

def reference(L0_attn_x, L0_attn_W_q, L0_attn_W_k, L0_attn_W_v, L0_attn_W_o, L0_attn_gn_weight, L0_attn_gn_bias, L0_ffn_t_emb, L0_ffn_sw1, L0_ffn_sb1, L0_ffn_sw3, L0_ffn_sb3, L0_ffn_sw2, L0_ffn_sb2, L0_ffn_w1, L0_ffn_b1, L0_ffn_w2, L0_ffn_b2):

    def _L0_attn_ref(x, W_q, W_k, W_v, W_o, gn_weight, gn_bias):
        import jax, jax.numpy as jnp
        import numpy as np
        D_MODEL = 256
        N_HEADS = 16
        D_HEAD = D_MODEL // N_HEADS
        B, T = (2, 512)
        EPS = 1e-05
        b, t, dm = x.shape
        h, dh = (N_HEADS, D_HEAD)
        gammas = 1.0 - 2.0 ** (-5.0 - jnp.arange(h, dtype=jnp.float32))
        q = (x @ W_q.T).reshape(b, t, h, dh)
        k = (x @ W_k.T).reshape(b, t, h, dh)
        v = (x @ W_v.T).reshape(b, t, h, dh)
        idx = jnp.arange(t)
        diff = idx[:, None] - idx[None, :]
        pow_ = jnp.maximum(diff, 0).astype(jnp.float32)
        decay = jnp.where(diff >= 0, gammas[:, None, None] ** pow_, 0.0)
        scale = jnp.sqrt(jnp.float32(dh))
        attn = jnp.einsum('bihd,bjhd->bhij', q, k) * decay[None] / scale
        y = jnp.einsum('bhij,bjhd->bihd', attn, v)
        mean = y.mean(axis=(1, 3), keepdims=True)
        var = y.var(axis=(1, 3), keepdims=True)
        yn = (y - mean) / jnp.sqrt(var + EPS)
        yn = yn.reshape(b, t, dm) * gn_weight + gn_bias
        return yn @ W_o.T

    def _L0_ffn_ref(x, t_emb, sw1, sb1, sw3, sb3, sw2, sb2, w1, b1, w2, b2):
        import jax, jax.numpy as jnp
        import numpy as np
        E = 8
        TOPK = 2
        PRIME = 11
        HASH_OFF = 7919
        N_SHARED = 1
        B, T, C = x.shape
        N = B * T
        xf = x.reshape(N, C)
        shared = jax.nn.silu(xf @ sw1 + sb1) * (xf @ sw3 + sb3) @ sw2 + sb2
        tok = jnp.arange(N)
        out = jnp.zeros((N, C), x.dtype)
        for k in range(TOPK):
            exp_ids = (tok * PRIME + k * HASH_OFF) % E
            sort_idx = jnp.argsort(exp_ids)
            xs = xf[sort_idx].reshape(E, N // E, C)
            h = jax.nn.gelu(jnp.einsum('enc,ech->enh', xs, w1) + b1[:, None, :], approximate=False)
            y = jnp.einsum('enh,ehc->enc', h, w2) + b2[:, None, :]
            out = out.at[sort_idx].add(y.reshape(N, C))
        out = out / TOPK
        return ((shared + out) / (N_SHARED + 1)).reshape(B, T, C)
    x = L0_attn_x
    x = x + _L0_attn_ref(_layernorm(x, axis=-1), L0_attn_W_q, L0_attn_W_k, L0_attn_W_v, L0_attn_W_o, L0_attn_gn_weight, L0_attn_gn_bias)
    x = x + _L0_ffn_ref(_layernorm(x, axis=-1), L0_ffn_t_emb, L0_ffn_sw1, L0_ffn_sb1, L0_ffn_sw3, L0_ffn_sb3, L0_ffn_sw2, L0_ffn_sb2, L0_ffn_w1, L0_ffn_b1, L0_ffn_w2, L0_ffn_b2)
    return x

_drawn_inputs = setup_inputs


def setup_inputs(seed=0):
    import zlib

    import numpy as np

    out = dict(_drawn_inputs(seed))
    spreads = {'L0_attn_gn_weight': (1.0, 0.2),
     'L0_attn_gn_bias': (0.0, 0.1),
     'L0_ffn_sb1': (0.0, 0.375),
     'L0_ffn_sb3': (0.0, 0.393),
     'L0_ffn_sb2': (0.0, 0.1),
     'L0_ffn_b1': (0.0, 0.503),
     'L0_ffn_b2': (0.0, 0.341)}
    factors = {}
    for name, (base, spread) in spreads.items():
        noise = np.random.default_rng([zlib.crc32(name.encode()), seed]).standard_normal(out[name].shape)
        drawn = base * np.exp(spread * noise) if base else spread * noise
        out[name] = jnp.asarray(drawn.astype(out[name].dtype))
    for name, factor in factors.items():
        out[name] = (out[name] * factor).astype(out[name].dtype)
    return out
```

```python
from contextlib import ExitStack

import concourse.bass as bass
from concourse import mybir

F32 = mybir.dt.float32
F32R = mybir.dt.float32r
ALU = mybir.AluOpType
ACT = mybir.ActivationFunctionType

P = 128
NBATCH, T, D = 4, 1024, 256
CB = D // P
NH, DH = 16, 16
EPS = 1e-5
SUPER = 256
NSUP = T // SUPER
TILES = SUPER // P
CH = 64
CPS = SUPER // CH
CPB = T // CH
GROUPS = NH * DH // P
PAIRS = 4
NE = 8
HS, HR = 512, 256
MS, MR = HS // P, HR // P
HALF = T // 2
ORDER = [NE - 1] + list(range(NE - 1))
MASK_COLS = dict(ident=(0, P), blockmask=(P, 2 * P), headmean=(2 * P, 3 * P), causal=(3 * P, 3 * P + CH),
                  parity=(3 * P + CH, 3 * P + CH + 2), pair=(3 * P + CH + 2, 3 * P + CH + 2 + PAIRS))
MASK_W = 3 * P + CH + 2 + PAIRS


def moe_retention(nc, xa, xs, wattn, gnw, gnb, sw1, sw3, sw2, w1, w2, sb1, sb3, b1, sb2, b2, decay, masks, out):
    x1_dram = nc.dram_tensor("x1_scratch", [NBATCH, P, NE * D], F32).ap()

    with ExitStack() as ctx:
        def sem(name):
            return ctx.enter_context(nc.semaphore(name))

        banks = [ctx.enter_context(nc.psum_tensor(f"bank{i}", [P, 512], F32)) for i in range(8)]
        phase1(nc, banks, sem, x1_dram, xa, xs, wattn, gnw, gnb, decay, masks)
        phase2(nc, banks, sem, x1_dram, sw1, sw3, sw2, w1, w2, sb1, sb3, b1, sb2, b2, masks, out)


def ahead(b, s, k):
    return b + (s + k) // NSUP, (s + k) % NSUP


def phase1(nc, banks, sem, x1_dram, xa, xs, wattn, gnw, gnb, decay, masks):
    p_bank, s_bank, y_bank = banks[0:2], banks[2], banks[3:5]
    a_bank, b_bank, c_bank = banks[5:8]
    out_bank = [banks[0], banks[1], banks[3], banks[4]]

    with ExitStack() as ctx:
        def sb(name, shape, dt=F32):
            return ctx.enter_context(nc.sbuf_tensor(name, shape, dt))

        wraw = sb("wraw", [P, 4, CB, D])
        whi = sb("whi", [P, 4, CB, D], F32R)
        wlo = sb("wlo", [P, 4, CB, D], F32R)
        dec = sb("dec", [P, 2, GROUPS, T])
        msk = sb("msk", [P, MASK_W])
        gn_w = sb("gn_w", [P, GROUPS])
        gn_b = sb("gn_b", [P, GROUPS])
        minus_half = sb("minus_half", [P, 2])
        xin = [sb(f"xin{i}", [P, TILES, D]) for i in range(NSUP)]
        ln_st = sb("ln_st", [P, TILES, 6])
        ln_mv = sb("ln_mv", [P, TILES, 2])
        ln_ve = sb("ln_ve", [P, TILES])
        ln_r = sb("ln_r", [P, TILES])
        xhi = sb("xhi", [P, CB, SUPER], F32R)
        xlo = sb("xlo", [P, CB, SUPER], F32R)
        qT = [sb(f"qT{i}", [P, GROUPS, SUPER]) for i in range(2)]
        kT = [sb(f"kT{i}", [P, GROUPS, SUPER]) for i in range(2)]
        qexp = [sb(f"qexp{i}", [P, CPS, GROUPS, PAIRS, CH]) for i in range(2)]
        keo = [sb(f"keo{i}", [P, CPS, GROUPS, 2, CH]) for i in range(2)]
        ktok = [sb(f"ktok{i}", [P, TILES, GROUPS, P]) for i in range(2)]
        vtok = [sb(f"vtok{i}", [P, TILES, GROUPS, P]) for i in range(2)]
        vexp = [sb(f"vexp{i}", [P, CPS, GROUPS * PAIRS, 32]) for i in range(2)]
        pm = [sb(f"pm{i}", [P, 2 * PAIRS, CH]) for i in range(2)]
        state = [sb(f"state{i}", [P, GROUPS, P]) for i in range(2)]
        yT = sb("yT", [P, GROUPS, T])
        y_st = sb("y_st", [P, GROUPS, NSUP, 6])
        y_mv = sb("y_mv", [P, GROUPS, 2])
        y_mh = sb("y_mh", [P, GROUPS])
        y_d = sb("y_d", [P, GROUPS])
        y_dd = sb("y_dd", [P, GROUPS])
        y_e = sb("y_e", [P, GROUPS])
        y_ve = sb("y_ve", [P, GROUPS])
        y_r = sb("y_r", [P, GROUPS])
        y_a = sb("y_a", [P, GROUPS])
        y_ma = sb("y_ma", [P, GROUPS])
        y_b = sb("y_b", [P, GROUPS])
        yn = sb("yn", [P, GROUPS, T])
        yhi = sb("yhi", [P, GROUPS, T], F32R)
        ylo = sb("ylo", [P, GROUPS, T], F32R)
        xres = sb("xres", [P, NE, D])

        def const(name):
            return msk[:, slice(*MASK_COLS[name])]

        ident, blockmask, headmean, causal, parity, pair = (
            const(n) for n in ("ident", "blockmask", "headmean", "causal", "parity", "pair"))

        x_landed = [sem(f"x_landed{i}") for i in range(NSUP)]
        w_landed, dec_landed, msk_landed, gn_landed = (sem(n) for n in ("w_landed", "dec_landed", "msk_landed", "gn_landed"))
        xres_landed, x1_stored = sem("xres_landed"), sem("x1_stored")
        whi_ready, wlo_ready, cleared, half_set = (sem(n) for n in ("whi_ready", "wlo_ready", "cleared", "half_set"))
        dve_passed, pool_passed = sem("dve_passed"), sem("pool_passed")
        ln_stats, ln_aggr, ln_var, ln_rstd, xn_ready = (sem(n) for n in ("ln_stats", "ln_aggr", "ln_var", "ln_rstd", "xn_ready"))
        t_done, xhi_ready, xlo_ready = sem("t_done"), sem("xhi_ready"), sem("xlo_ready")
        q_done, k_done, v_done, kt_done = (sem(n) for n in ("q_done", "k_done", "v_done", "kt_done"))
        qT_ready, kT_ready, v_copied, ktok_copied, qk_ready = (
            sem(n) for n in ("qT_ready", "kT_ready", "v_copied", "ktok_copied", "qk_ready"))
        sc_done, pm_ready, y_done, y_copied, s_done, s_ready = (
            sem(n) for n in ("sc_done", "pm_ready", "y_done", "y_copied", "s_done", "s_ready"))
        y_stats, gn_aggr, gn_mean, gn_dev, gn_sq, gn_e, gn_var = (
            sem(n) for n in ("y_stats", "gn_aggr", "gn_mean", "gn_dev", "gn_sq", "gn_e", "gn_var"))
        gn_ve, gn_rstd, gn_a, gn_ma, gn_ready = (sem(n) for n in ("gn_ve", "gn_rstd", "gn_a", "gn_ma", "gn_ready"))
        yn_ready, yhi_ready, ylo_ready, o_done, x1_ready = (
            sem(n) for n in ("yn_ready", "yhi_ready", "ylo_ready", "o_done", "x1_ready"))

        block = ctx.enter_context(nc.Block())

        @block.sync
        def _(sp):
            sp.dma_start(xin[0][:], xa[0]).then_inc(x_landed[0], 16)
            sp.dma_start(msk[:], masks).then_inc(msk_landed, 16)
            sp.dma_start(wraw[:], wattn).then_inc(w_landed, 16)
            for s in range(1, NSUP):
                sp.dma_start(xin[s][:], xa[s]).then_inc(x_landed[s], 16)
            sp.dma_start(dec[:], decay).then_inc(dec_landed, 16)
            sp.dma_start(gn_w[:], gnw).then_inc(gn_landed, 16)
            sp.dma_start(gn_b[:], gnb).then_inc(gn_landed, 16)
            sp.dma_start(xres[:], xs[0]).then_inc(xres_landed, 16)

            def store(b):
                sp.wait_ge(x1_ready, (b + 1) * 4)
                sp.dma_start(x1_dram[b], xres[:]).then_inc(x1_stored, 16)
                sp.wait_ge(x1_stored, (b + 1) * 16)

            with sp.Fori(0, NBATCH - 1) as b:
                for s in range(NSUP):
                    sp.wait_ge(t_done, b * NSUP + (s + 1))
                    sp.dma_start(xin[s][:], xa[b * NSUP + (NSUP + s)]).then_inc(x_landed[s], 16)
                store(b)
                sp.dma_start(xres[:], xs[b + 1]).then_inc(xres_landed, 16)
            store(NBATCH - 1)

        @block.tensor
        def _(pe):
            def split_product(o, w, x, first=True, last=True):
                n = len(w)
                for c in range(n):
                    for j, (l, r) in enumerate(((0, 0), (1, 0), (0, 1))):
                        mm = nc.tensor.matmul(o, w[c][l], x[c][r], start=first and c == 0 and j == 0,
                                              stop=last and c == n - 1 and j == 2)
                return mm

            def transpose_x(b, s):
                h = b * NSUP + s
                pe.wait_ge(xn_ready, h + 1)
                if not (isinstance(h, int) and h == 0):
                    pe.wait_ge(v_copied, h)
                for c in range(CB):
                    for t in range(TILES):
                        mm = nc.tensor.transpose(a_bank[:, c * SUPER + t * P:c * SUPER + (t + 1) * P],
                                                 xin[s][:, t, c * P:(c + 1) * P], ident)
                mm.then_inc(t_done, 1)

            def project(b, s, between=(None, None)):
                h = b * NSUP + s
                static0 = isinstance(h, int) and h == 0
                x = [(xhi[:, c, :], xlo[:, c, :]) for c in range(CB)]
                pe.wait_ge(xlo_ready, h + 1)
                for i, (bank, done) in enumerate(((b_bank, q_done), (c_bank, k_done))):
                    if not static0:
                        pe.wait_ge((ktok_copied, kT_ready)[i], h)
                    for g in range(GROUPS):
                        w = [(whi[:, i, c, g * P:(g + 1) * P], wlo[:, i, c, g * P:(g + 1) * P]) for c in range(CB)]
                        mm = split_product(bank[:, g * SUPER:(g + 1) * SUPER], w, x)
                    mm.then_inc(done, 1)
                    if between[i]:
                        between[i]()
                for t in range(TILES):
                    w = [(xhi[:, c, t * P:(t + 1) * P], xlo[:, c, t * P:(t + 1) * P]) for c in range(CB)]
                    mm = split_product(a_bank[:, t * D:(t + 1) * D], w, [(whi[:, 2, c, :], wlo[:, 2, c, :]) for c in range(CB)])
                mm.then_inc(v_done, 1)

            def k_by_tokens(b, s):
                h = b * NSUP + s
                pe.wait_ge(kT_ready, h + 1)
                pe.wait_ge(qT_ready, h + 1)
                for t in range(TILES):
                    for g in range(GROUPS):
                        o = (t * GROUPS + g) * P
                        mm = nc.tensor.transpose(b_bank[:, o:o + P], kT[s % 2][:, g, t * P:(t + 1) * P], ident)
                mm.then_inc(kt_done, 1)

            def scores(b, s, c):
                n = (b * NSUP + s) * CPS + c
                if c == 0:
                    pe.wait_ge(qk_ready, b * NSUP + (s + 1))
                if not (isinstance(n, int) and n < 2):
                    pe.wait_ge(pm_ready, n - 1)
                for g in range(GROUPS):
                    mm = nc.tensor.matmul(p_bank[c % 2][:, g * PAIRS * CH:(g + 1) * PAIRS * CH],
                                          keo[s % 2][:, c, g, :, :], qexp[s % 2][:, c, g, :, :], start=True, stop=True)
                mm.then_inc(sc_done, 1)

            def retain(b, s, c):
                n = (b * NSUP + s) * CPS + c
                m = s * CPS + c
                if not (isinstance(n, int) and n < 2):
                    pe.wait_ge(y_copied, n - 1)
                if m > 0:
                    pe.wait_ge(s_ready, b * (CPB - 1) + m)
                    for g in range(GROUPS):
                        nc.tensor.matmul(y_bank[c % 2][:, g * CH:(g + 1) * CH], state[(c + 1) % 2][:, g, :],
                                         qT[s % 2][:, g, c * CH:(c + 1) * CH], start=(g == 0), stop=False,
                                         skip_group_check=True)
                if c == 0:
                    pe.wait_ge(v_copied, b * NSUP + (s + 1))
                pe.wait_ge(pm_ready, n + 1)
                for g in range(GROUPS):
                    for p in range(PAIRS):
                        mm = nc.tensor.matmul(y_bank[c % 2][32 * p:32 * p + 32, g * CH:(g + 1) * CH],
                                              vexp[s % 2][:, c, g * PAIRS + p, :], pm[c % 2][:, g * PAIRS + p, :],
                                              start=(m == 0 and g == 0), stop=True, skip_group_check=True)
                mm.then_inc(y_done, 1)
                if m == CPB - 1:
                    return
                if m == 0 and not (isinstance(b, int) and b == 0):
                    pe.wait_ge(gn_ready, b)
                if c == 0:
                    pe.wait_ge(ktok_copied, b * NSUP + (s + 1))
                t, lo = c // 2, (c % 2) * CH
                for g in range(GROUPS):
                    mm = nc.tensor.matmul(s_bank[:, g * P:(g + 1) * P], ktok[s % 2][lo:lo + CH, t, g, :],
                                          vtok[s % 2][lo:lo + CH, t, g, :], start=(m == 0 and g == 0), stop=True,
                                          skip_group_check=True)
                mm.then_inc(s_done, 1)

            def head_means(b):
                pe.wait_ge(gn_aggr, b + 1)
                nc.tensor.matmul(s_bank[:, 0:GROUPS], headmean, y_mv[:, :, 0], start=True, stop=True).then_inc(gn_mean, 1)

            def head_vars(b):
                pe.wait_ge(gn_e, b + 1)
                nc.tensor.matmul(s_bank[:, 8:8 + GROUPS], headmean, y_e[:], start=True, stop=True).then_inc(gn_var, 1)

            def output(b):
                pe.wait_ge(ylo_ready, (b + 1) * GROUPS)
                n = (b + 1) * CPB if isinstance(b, int) and b == NBATCH - 1 else (b + 1) * CPB + CPS
                pe.wait_ge(pm_ready, n)
                pe.wait_ge(y_copied, n)
                for j in range(4):
                    for i in range(2):
                        at = (2 * j + i) * P
                        w = [(yhi[:, c, at:at + P], ylo[:, c, at:at + P]) for c in range(CB)]
                        mm = split_product(out_bank[j][:, i * D:(i + 1) * D], w,
                                           [(whi[:, 3, c, :], wlo[:, 3, c, :]) for c in range(CB)])
                    mm.then_inc(o_done, 1)

            def step(b, s, norm=False):
                static = isinstance(b, int)
                g = b * NSUP + s
                if not (static and g + 1 >= NBATCH * NSUP):
                    project(*ahead(b, s, 1), between=(lambda: head_means(b - 1), lambda: head_vars(b - 1)) if norm else (None, None))
                if not (static and g + 2 >= NBATCH * NSUP):
                    transpose_x(*ahead(b, s, 2))
                scores(b, s, 0)
                if not (static and g + 1 >= NBATCH * NSUP):
                    k_by_tokens(*ahead(b, s, 1))
                for c in range(CPS):
                    if c + 1 < CPS:
                        scores(b, s, c + 1)
                    retain(b, s, c)
                if norm:
                    output(b - 1)
                    pe.wait_ge(x1_ready, b * 4)

            pe.wait_ge(msk_landed, 16)
            transpose_x(0, 0)
            pe.wait_ge(wlo_ready, 4)
            project(0, 0)
            transpose_x(0, 1)
            k_by_tokens(0, 0)
            step(0, 0)
            with pe.Fori(0, NBATCH - 1) as b:
                for s in range(1, NSUP):
                    step(b, s)
                step(b + 1, 0, norm=True)
            for s in range(1, NSUP):
                step(NBATCH - 1, s)
            head_means(NBATCH - 1)
            head_vars(NBATCH - 1)
            output(NBATCH - 1)

        @block.scalar
        def _(act):
            def high_x(b, s):
                h = b * NSUP + s
                act.wait_ge(t_done, h + 1)
                nc.scalar.activation(xhi[:].rearrange("p c t -> p (c t)"), a_bank[:], ACT.Copy).then_inc(xhi_ready, 1)

            def copy_v(b, s):
                h = b * NSUP + s
                act.wait_ge(v_done, h + 1)
                nc.scalar.activation(vtok[s % 2][:].rearrange("p t g n -> p (t g n)"), a_bank[:], ACT.Copy)
                src = a_bank[:].rearrange("p (t r h e) -> p t r h e", t=TILES, h=2, e=DH)
                dst = vexp[s % 2][:].rearrange("p (t f) r (h e) -> p t f r h e", f=2, h=2)
                for f in range(2):
                    for h2 in range(2):
                        last = nc.scalar.activation(dst[64 * h2:64 * h2 + 64, :, f, :, h2, :],
                                                    src[64 * f:64 * f + 64, :, :, h2, :], ACT.Copy)
                last.then_inc(v_copied, 1)

            def copy_k(b, s):
                h = b * NSUP + s
                act.wait_ge(kt_done, h + 1)
                nc.scalar.activation(ktok[s % 2][:].rearrange("p t g n -> p (t g n)"), b_bank[:], ACT.Copy).then_inc(ktok_copied, 1)

            def copy_y(b, s, c):
                n = (b * NSUP + s) * CPS + c
                m = s * CPS + c
                act.wait_ge(y_done, n + 1)
                nc.scalar.activation(yT[:, :, m * CH:(m + 1) * CH],
                                     y_bank[c % 2][:, 0:GROUPS * CH].rearrange("p (g i) -> p g i", g=GROUPS),
                                     ACT.Copy).then_inc(y_copied, 1)

            def normalise_y(b):
                act.wait_ge(gn_ready, b + 1)
                for g in range(GROUPS):
                    nc.scalar.activation(yn[:, g, :].rearrange("p (s k u) -> p s k u", s=NE, k=CPB),
                                         yT[:, g, :].rearrange("p (k s u) -> p s k u", s=NE, k=CPB),
                                         ACT.Identity, bias=y_b[:, g:g + 1], scale=y_a[:, g:g + 1]).then_inc(yn_ready, 1)
                for g in range(GROUPS):
                    act.wait_ge(yn_ready, b * GROUPS + (g + 1))
                    nc.scalar.activation(yhi[:, g, :], yn[:, g, :], ACT.Copy).then_inc(yhi_ready, 1)

            def step(b, s, norm=False):
                static = isinstance(b, int)
                g = b * NSUP + s
                if not (static and g + 1 >= NBATCH * NSUP):
                    copy_v(*ahead(b, s, 1))
                if not (static and g + 2 >= NBATCH * NSUP):
                    high_x(*ahead(b, s, 2))
                if norm:
                    normalise_y(b - 1)
                if not (static and g + 1 >= NBATCH * NSUP):
                    copy_k(*ahead(b, s, 1))
                for c in range(CPS):
                    copy_y(b, s, c)

            high_x(0, 0)
            act.wait_ge(w_landed, 16)
            for i in range(4):
                nc.scalar.activation(whi[:, i], wraw[:, i], ACT.Copy).then_inc(whi_ready, 1)
            act.wait_ge(cleared, 2)
            copy_v(0, 0)
            high_x(0, 1)
            copy_k(0, 0)
            step(0, 0)
            with act.Fori(0, NBATCH - 1) as b:
                for s in range(1, NSUP):
                    step(b, s)
                step(b + 1, 0, norm=True)
            for s in range(1, NSUP):
                step(NBATCH - 1, s)
            normalise_y(NBATCH - 1)

        @block.vector
        def _(dve):
            def passed(s, value):
                dve.wait_ge(s, value)
                dve.sem_inc(dve_passed, 1)

            def ln_sums(b, s):
                h = b * NSUP + s
                dve.wait_ge(x_landed[s], (b + 1) * 16)
                for t in range(TILES):
                    st = nc.vector.bn_stats(ln_st[:, t, :], xin[s][:, t, :])
                st.then_inc(ln_stats, 1)
                passed(ln_stats, h + 1)
                for t in range(TILES):
                    ag = nc.vector.bn_aggr(ln_mv[:, t, :], ln_st[:, t, :])
                ag.then_inc(ln_aggr, 1)
                dve.wait_ge(ln_aggr, h + 1)
                nc.vector.tensor_scalar(ln_ve[:], ln_mv[:, :, 1], EPS, None, ALU.add).then_inc(ln_var, 1)

            def ln_apply(b, s):
                h = b * NSUP + s
                dve.wait_ge(ln_rstd, h + 1)
                for t in range(TILES):
                    ts = nc.vector.tensor_scalar(xin[s][:, t, :], xin[s][:, t, :], ln_mv[:, t, 0:1], ln_r[:, t:t + 1],
                                                 ALU.subtract, ALU.mult)
                ts.then_inc(xn_ready, 1)

            def low_x(b, s):
                h = b * NSUP + s
                dve.wait_ge(xhi_ready, h + 1)
                nc.vector.tensor_tensor(xlo[:].rearrange("p c t -> p (c t)"), a_bank[:],
                                        xhi[:].rearrange("p c t -> p (c t)").bitcast(F32), ALU.subtract).then_inc(xlo_ready, 1)

            def decay_qk(b, s, i):
                h = b * NSUP + s
                dst, bank, done, ready = ((qT, b_bank, q_done, qT_ready), (kT, c_bank, k_done, kT_ready))[i]
                dve.wait_ge(done, h + 1)
                nc.vector.tensor_tensor(dst[s % 2][:], bank[:].rearrange("p (g t) -> p g t", g=GROUPS),
                                        dec[:, i, :, s * SUPER:(s + 1) * SUPER], ALU.mult).then_inc(ready, 1)

            def mask_scores(b, s, c):
                n = (b * NSUP + s) * CPS + c
                dve.wait_ge(sc_done, n + 1)
                nc.vector.tensor_tensor(pm[c % 2][:], p_bank[c % 2][:].rearrange("p (a i) -> p a i", i=CH),
                                        causal.unsqueeze(1).broadcast_to([P, 2 * PAIRS, CH]), ALU.mult).then_inc(pm_ready, 1)

            def mask_state(b, s, c):
                m = s * CPS + c
                if m == CPB - 1:
                    return
                dve.wait_ge(s_done, b * (CPB - 1) + (m + 1))
                nc.vector.tensor_tensor(state[c % 2][:], s_bank[:, 0:GROUPS * P].rearrange("p (g e) -> p g e", g=GROUPS),
                                        blockmask.unsqueeze(1).broadcast_to([P, GROUPS, P]), ALU.mult).then_inc(s_ready, 1)

            def y_sums(b, s):
                dve.wait_ge(y_copied, (b * NSUP + (s + 1)) * CPS)
                for g in range(GROUPS):
                    st = nc.vector.bn_stats(y_st[:, g, s, :], yT[:, g, s * SUPER:(s + 1) * SUPER])
                st.then_inc(y_stats, 1)

            def gn_channels(b):
                passed(y_stats, (b + 1) * NSUP)
                for g in range(GROUPS):
                    ag = nc.vector.bn_aggr(y_mv[:, g, :], y_st[:, g, :, :].rearrange("p s k -> p (s k)"))
                ag.then_inc(gn_aggr, 1)

            def gn_spread(b):
                dve.wait_ge(gn_mean, b + 1)
                nc.vector.tensor_copy(y_mh[:], s_bank[:, 0:GROUPS])
                nc.vector.tensor_tensor(y_d[:], s_bank[:, 0:GROUPS], y_mv[:, :, 0], ALU.subtract).then_inc(gn_dev, 1)
                dve.wait_ge(gn_dev, b + 1)
                nc.vector.tensor_tensor(y_dd[:], y_d[:], y_d[:], ALU.mult).then_inc(gn_sq, 1)
                dve.wait_ge(gn_sq, b + 1)
                nc.vector.tensor_tensor(y_e[:], y_dd[:], y_mv[:, :, 1], ALU.add).then_inc(gn_e, 1)

            def gn_eps(b):
                dve.wait_ge(gn_var, b + 1)
                nc.vector.tensor_scalar(y_ve[:], s_bank[:, 8:8 + GROUPS], EPS, None, ALU.add).then_inc(gn_ve, 1)

            def gn_affine(b):
                dve.wait_ge(gn_rstd, b + 1)
                nc.vector.tensor_tensor(y_a[:], y_r[:], gn_w[:], ALU.mult).then_inc(gn_a, 1)
                dve.wait_ge(gn_a, b + 1)
                nc.vector.tensor_tensor(y_ma[:], y_mh[:], y_a[:], ALU.mult).then_inc(gn_ma, 1)
                dve.wait_ge(gn_ma, b + 1)
                nc.vector.tensor_tensor(y_b[:], gn_b[:], y_ma[:], ALU.subtract).then_inc(gn_ready, 1)

            def low_y(b):
                for g in range(GROUPS):
                    dve.wait_ge(yhi_ready, b * GROUPS + (g + 1))
                    nc.vector.tensor_tensor(ylo[:, g, :], yn[:, g, :], yhi[:, g, :].bitcast(F32), ALU.subtract).then_inc(ylo_ready, 1)

            def residual(b):
                dve.wait_ge(xres_landed, (b + 1) * 16)
                for j in range(4):
                    dve.wait_ge(o_done, b * 4 + (j + 1))
                    part = xres[:, 2 * j:2 * j + 2, :].rearrange("p s d -> p (s d)")
                    nc.vector.tensor_tensor(part, out_bank[j][:], part, ALU.add).then_inc(x1_ready, 1)

            def step(b, s, norm=False):
                static = isinstance(b, int)
                g = b * NSUP + s
                more = [not (static and g + k >= NBATCH * NSUP) for k in range(4)]
                if not (static and g == 0):
                    y_sums(*ahead(b - 1, s, 3))
                if norm:
                    gn_channels(b - 1)
                if more[3]:
                    ln_sums(*ahead(b, s, 3))
                if more[1]:
                    decay_qk(*ahead(b, s, 1), 0)
                if norm:
                    gn_spread(b - 1)
                if more[1]:
                    decay_qk(*ahead(b, s, 1), 1)
                if norm:
                    gn_eps(b - 1)
                if more[2]:
                    low_x(*ahead(b, s, 2))
                if norm:
                    gn_affine(b - 1)
                if more[3]:
                    ln_apply(*ahead(b, s, 3))
                for c in range(CPS):
                    mask_scores(b, s, c)
                    mask_state(b, s, c)
                if norm:
                    low_y(b - 1)
                    residual(b - 1)

            for i in range(2):
                nc.vector.memset(vexp[i][:], 0.0).then_inc(cleared, 1)
            ln_sums(0, 0)
            ln_apply(0, 0)
            ln_sums(0, 1)
            ln_apply(0, 1)
            low_x(0, 0)
            for i in range(4):
                dve.wait_ge(whi_ready, i + 1)
                nc.vector.tensor_tensor(wlo[:, i], wraw[:, i], whi[:, i].bitcast(F32), ALU.subtract).then_inc(wlo_ready, 1)
            dve.wait_ge(dec_landed, 16)
            decay_qk(0, 0, 0)
            decay_qk(0, 0, 1)
            low_x(0, 1)
            ln_sums(0, 2)
            ln_apply(0, 2)
            dve.wait_ge(gn_landed, 32)
            step(0, 0)
            with dve.Fori(0, NBATCH - 1) as b:
                for s in range(1, NSUP):
                    step(b, s)
                step(b + 1, 0, norm=True)
            for s in range(1, NSUP):
                step(NBATCH - 1, s)
            last = NBATCH - 1
            y_sums(last, NSUP - 1)
            gn_channels(last)
            gn_spread(last)
            gn_eps(last)
            gn_affine(last)
            low_y(last)
            residual(last)

        @block.gpsimd
        def _(pool):
            def passed(s, value):
                pool.wait_ge(s, value)
                pool.sem_inc(pool_passed, 1)

            def ln_power(b, s):
                pool.wait_ge(ln_var, b * NSUP + (s + 1))
                nc.gpsimd.tensor_tensor(ln_r[:], ln_ve[:], minus_half[:], ALU.pow).then_inc(ln_rstd, 1)

            def gn_power(b):
                pool.wait_ge(gn_ve, b + 1)
                nc.gpsimd.tensor_tensor(y_r[:], y_ve[:], minus_half[:], ALU.pow).then_inc(gn_rstd, 1)

            def spread_qk(b, s):
                h = b * NSUP + s
                passed(qT_ready, h + 1)
                q = qT[s % 2][:].rearrange("p g (c i) -> p c g i", c=CPS)
                for p in range(PAIRS):
                    nc.gpsimd.tensor_scalar(qexp[s % 2][:, :, :, p, :], q, pair[:, p:p + 1], None, ALU.mult)
                passed(kT_ready, h + 1)
                k = kT[s % 2][:].rearrange("p g (c j) -> p c g j", c=CPS)
                for odd in range(2):
                    last = nc.gpsimd.tensor_scalar(keo[s % 2][:, :, :, odd, :], k, parity[:, odd:odd + 1], None, ALU.mult)
                last.then_inc(qk_ready, 1)

            def step(b, s, norm=False):
                static = isinstance(b, int)
                g = b * NSUP + s
                if not (static and g + 3 >= NBATCH * NSUP):
                    ln_power(*ahead(b, s, 3))
                if norm:
                    gn_power(b - 1)
                if not (static and g + 1 >= NBATCH * NSUP):
                    spread_qk(*ahead(b, s, 1))

            nc.gpsimd.memset(minus_half[:], -0.5).then_inc(half_set, 1)
            pool.wait_ge(half_set, 1)
            ln_power(0, 0)
            ln_power(0, 1)
            pool.wait_ge(msk_landed, 16)
            spread_qk(0, 0)
            ln_power(0, 2)
            step(0, 0)
            with pool.Fori(0, NBATCH - 1) as b:
                for s in range(1, NSUP):
                    step(b, s)
                step(b + 1, 0, norm=True)
            for s in range(1, NSUP):
                step(NBATCH - 1, s)
            gn_power(NBATCH - 1)


def phase2(nc, banks, sem, x1_dram, sw1, sw3, sw2, w1, w2, sb1, sb3, b1, sb2, b2, masks, out):
    h1_bank, h3_bank, e_bank, o_bank = (banks[0], banks[2]), (banks[1], banks[3]), banks[4:6], banks[6:8]
    t2_bank = banks[0:4]

    with ExitStack() as ctx:
        def sb(name, shape, dt=F32):
            return ctx.enter_context(nc.sbuf_tensor(name, shape, dt))

        def split_weight(name, shape):
            hi = sb(name + "_hi", shape, F32R)
            with nc.sbuf_tensor(name + "_raw", shape, F32) as raw:
                pass
            lo = sb(name + "_lo", shape, F32R)
            return hi, lo, raw

        s1hi, s1lo, s1raw = split_weight("sw1", [P, CB, HS])
        s3hi, s3lo, s3raw = split_weight("sw3", [P, CB, HS])
        r1hi, r1lo, r1raw = split_weight("w1", [P, NE, CB, HR])
        s2hi, s2lo, s2raw = split_weight("sw2", [P, MS, D])
        r2hi, r2lo, r2raw = split_weight("w2", [P, NE, MR, D])
        ident = sb("ident2", [P, P])
        s1b = sb("s1b", [P, MS])
        s3b = sb("s3b", [P, MS])
        r1b = sb("r1b", [P, NE, MR])
        bias = sb("bias", [P, NE, D])
        sbias = sb("sbias", [P, D])
        bias7 = sb("bias7", [P, D])
        minus_half = sb("minus_half2", [P, 4])
        xl = sb("xl", [P, NE, D])
        xr = sb("xr", [P, NE, D])
        st = sb("ln2_st", [P, 4, 6])
        mv = sb("ln2_mv", [P, 4, 2])
        ve = sb("ln2_ve", [P, 4])
        rs = sb("ln2_r", [P, 4])
        xn = sb("xn2", [P, NE, D])
        xhi = sb("x2hi", [P, CB, T + P], F32R)
        xlo = sb("x2lo", [P, CB, T + P], F32R)
        sil = [sb(f"sil{i}", [P, HALF]) for i in range(2)]
        gf = [sb(f"gf{i}", [P, HALF]) for i in range(3)]
        ghi = sb("ghi", [P, MS, T], F32R)
        glo = sb("glo", [P, MS, T], F32R)
        hf = [sb(f"hf{i}", [P, MR, 2 * P]) for i in range(2)]
        ehi = [sb(f"ehi{i}", [P, MR, 2 * P], F32R) for i in range(4)]
        elo = [sb(f"elo{i}", [P, MR, 2 * P], F32R) for i in range(4)]

        def expert_buffer(e):
            return 3 if e == NE - 1 else e % 3

        names = ("sw1", "sw3", "w1", "sw2", "w2")
        landed = {n: sem(n + "_landed") for n in names}
        c2_landed, bias_landed, xl_landed, xr_landed, stored = (
            sem(n) for n in ("c2_landed", "bias_landed", "xl_landed", "xr_landed", "stored"))
        hi_split, lo_split, bias_ready, bias_part, half2_set = (
            sem(n) for n in ("hi_split", "lo_split", "bias_ready", "bias_part", "half2_set"))
        dve2_passed, pool2_passed = sem("dve2_passed"), sem("pool2_passed")
        ln2_stats, ln2_aggr, ln2_var, ln2_rstd, xn2_ready = (
            sem(n) for n in ("ln2_stats", "ln2_aggr", "ln2_var", "ln2_rstd", "xn2_ready"))
        t2_done, x2hi_ready, x2lo_ready = sem("t2_done"), sem("x2hi_ready"), sem("x2lo_ready")
        h1_done, h3_done, sil_ready, gf_ready, ghi_ready, glo_ready = (
            sem(n) for n in ("h1_done", "h3_done", "sil_ready", "gf_ready", "ghi_ready", "glo_ready"))
        e_done, gelu_ready, ehi_ready, elo_ready, slot_done, biased, o_ready = (
            sem(n) for n in ("e_done", "gelu_ready", "ehi_ready", "elo_ready", "slot_done", "biased", "o_ready"))

        block = ctx.enter_context(nc.Block())
        last_batch = NBATCH - 1

        @block.sync
        def _(sp):
            sp.dma_start(xl[:], x1_dram[0]).then_inc(xl_landed, 16)
            sp.dma_start(ident[:], masks[:, 0:P]).then_inc(c2_landed, 16)
            for dst, src in ((s1b, sb1), (s3b, sb3), (r1b, b1)):
                sp.dma_start(dst[:], src).then_inc(c2_landed, 16)
            for n, dst, src in zip(names, (s1raw, s3raw, r1raw, s2raw, r2raw), (sw1, sw3, w1, sw2, w2)):
                sp.dma_start(dst[:], src).then_inc(landed[n], 16)
            sp.dma_start(xr[:], x1_dram[0]).then_inc(xr_landed, 16)
            sp.dma_start(bias[:], b2.partition_broadcast(P)).then_inc(bias_landed, 16)
            sp.dma_start(sbias[:], sb2.partition_broadcast(P)).then_inc(bias_landed, 16)

            def store(b):
                for half in range(2):
                    sp.wait_ge(o_ready, b * NE + 4 * (half + 1))
                    at = slice(4 * half, 4 * half + 4)
                    sp.dma_start(out[b].rearrange("p (s d) -> p s d", s=NE)[:, at, :], xr[:, at, :]).then_inc(stored, 16)
                sp.wait_ge(stored, (b + 1) * 32)

            with sp.Fori(0, last_batch) as b:
                sp.wait_ge(xn2_ready, (b + 1) * 2)
                sp.dma_start(xl[:], x1_dram[b + 1]).then_inc(xl_landed, 16)
                store(b)
                sp.dma_start(xr[:], x1_dram[b + 1]).then_inc(xr_landed, 16)
            store(last_batch)

        @block.tensor
        def _(pe):
            def split_product(o, w, x, first=True, last=True):
                n = len(w)
                for c in range(n):
                    for j, (l, r) in enumerate(((0, 0), (1, 0), (0, 1))):
                        mm = nc.tensor.matmul(o, w[c][l], x[c][r], start=first and c == 0 and j == 0,
                                              stop=last and c == n - 1 and j == 2)
                return mm

            def transpose_x(b):
                if not (isinstance(b, int) and b == 0):
                    pe.wait_ge(sil_ready, b * 8)
                    pe.wait_ge(gf_ready, b * 8)
                for half in range(2):
                    pe.wait_ge(xn2_ready, b * 2 + (half + 1))
                    for c in range(CB):
                        for t in range(4):
                            mm = nc.tensor.transpose(t2_bank[2 * half + c][:, t * P:(t + 1) * P],
                                                     xn[:, 4 * half + t, c * P:(c + 1) * P], ident[:])
                        mm.then_inc(t2_done, 1)

            def shared(b):
                pe.wait_ge(x2lo_ready, b * 4 + 4)
                for half in range(2):
                    x = [(xhi[:, c, half * HALF:(half + 1) * HALF], xlo[:, c, half * HALF:(half + 1) * HALF]) for c in range(CB)]
                    for m in range(MS):
                        i = half * MS + m
                        for hi, lo, bank, done, read in ((s1hi, s1lo, h1_bank, h1_done, sil_ready),
                                                         (s3hi, s3lo, h3_bank, h3_done, gf_ready)):
                            if i >= 2:
                                pe.wait_ge(read, b * 8 + (i - 1))
                            w = [(hi[:, c, m * P:(m + 1) * P], lo[:, c, m * P:(m + 1) * P]) for c in range(CB)]
                            split_product(bank[m % 2][:], w, x).then_inc(done, 1)

            def expert(b, q):
                e = ORDER[q]
                if q >= 2:
                    pe.wait_ge(gelu_ready, b * NE + (q - 1))
                x = [(xhi[:, c, e * P:(e + 2) * P], xlo[:, c, e * P:(e + 2) * P]) for c in range(CB)]
                for m in range(MR):
                    w = [(r1hi[:, e, c, m * P:(m + 1) * P], r1lo[:, e, c, m * P:(m + 1) * P]) for c in range(CB)]
                    mm = split_product(e_bank[q % 2][:, m * 2 * P:(m + 1) * 2 * P], w, x)
                mm.then_inc(e_done, 1)

            def slot(b, s):
                if s in (0, 4):
                    pe.wait_ge(glo_ready, b * 8 + (s + 4))
                if s >= 2:
                    pe.wait_ge(o_ready, b * NE + (s - 1))
                g = [(ghi[:, m, s * P:(s + 1) * P], glo[:, m, s * P:(s + 1) * P]) for m in range(MS)]
                w = [(s2hi[:, m, :], s2lo[:, m, :]) for m in range(MS)]
                if s == 0:
                    pe.wait_ge(elo_ready, b * NE + 2)
                elif s < NE - 1:
                    pe.wait_ge(elo_ready, b * NE + (s + 2))
                for e, part in (((s - 1) % NE, 1), (s, 0)):
                    k = expert_buffer(e)
                    g += [(ehi[k][:, m, part * P:(part + 1) * P], elo[k][:, m, part * P:(part + 1) * P]) for m in range(MR)]
                    w += [(r2hi[:, e, m, :], r2lo[:, e, m, :]) for m in range(MR)]
                split_product(o_bank[s % 2][:, 0:D], g, w).then_inc(slot_done, 1)

            def batch(b, more):
                shared(b)
                if isinstance(b, int) and b == 0:
                    pe.wait_ge(lo_split, 5)
                expert(b, 0)
                expert(b, 1)
                for q in range(2, NE):
                    expert(b, q)
                    slot(b, q - 2)
                if more:
                    transpose_x(b + 1)
                slot(b, NE - 2)
                slot(b, NE - 1)

            pe.wait_ge(c2_landed, 64)
            transpose_x(0)
            pe.wait_ge(lo_split, 5)
            with pe.Fori(0, last_batch) as b:
                batch(b, True)
            batch(last_batch, False)

        @block.scalar
        def _(act):
            def high_x(b):
                for half in range(2):
                    for c in range(CB):
                        j = 2 * half + c
                        act.wait_ge(t2_done, b * 4 + (j + 1))
                        cp = nc.scalar.activation(xhi[:, c, half * HALF:(half + 1) * HALF], t2_bank[j][:], ACT.Copy)
                        if half == 0:
                            cp = nc.scalar.activation(xhi[:, c, T:T + P], t2_bank[j][:, 0:P], ACT.Copy)
                        cp.then_inc(x2hi_ready, 1)

            def batch(b, more):
                for i in range(2 * MS):
                    m = i % MS
                    act.wait_ge(h1_done, b * 8 + (i + 1))
                    if i >= 2:
                        act.wait_ge(gf_ready, b * 8 + (i - 1))
                    nc.scalar.activation(sil[i % 2][:], h1_bank[i % 2][:], ACT.Silu, bias=s1b[:, m:m + 1]).then_inc(sil_ready, 1)
                for q in range(NE):
                    e = ORDER[q]
                    act.wait_ge(e_done, b * NE + (q + 1))
                    if q >= 2:
                        act.wait_ge(elo_ready, b * NE + (q - 1))
                    for m in range(MR):
                        ge = nc.scalar.activation(hf[q % 2][:, m, :], e_bank[q % 2][:, m * 2 * P:(m + 1) * 2 * P], ACT.Gelu,
                                                  bias=r1b[:, e, m:m + 1])
                    ge.then_inc(gelu_ready, 1)
                if more:
                    high_x(b + 1)

            for n, hi, raw, scale in zip(names, (s1hi, s3hi, r1hi, s2hi, r2hi), (s1raw, s3raw, r1raw, s2raw, r2raw),
                                         (1.0, 1.0, 1.0, 0.5, 0.25)):
                act.wait_ge(landed[n], 16)
                nc.scalar.activation(hi[:], raw[:], ACT.Copy, scale=scale).then_inc(hi_split, 1)
                if n == "sw3":
                    high_x(0)
            with act.Fori(0, last_batch) as b:
                batch(b, True)
            batch(last_batch, False)

        @block.vector
        def _(dve):
            def passed(s, value):
                dve.wait_ge(s, value)
                dve.sem_inc(dve2_passed, 1)

            def ln_sums(b, half):
                if half == 0:
                    dve.wait_ge(xl_landed, (b + 1) * 16)
                for t in range(4):
                    bs = nc.vector.bn_stats(st[:, t, :], xl[:, 4 * half + t, :])
                bs.then_inc(ln2_stats, 1)
                passed(ln2_stats, b * 2 + (half + 1))
                for t in range(4):
                    ag = nc.vector.bn_aggr(mv[:, t, :], st[:, t, :])
                ag.then_inc(ln2_aggr, 1)
                dve.wait_ge(ln2_aggr, b * 2 + (half + 1))
                nc.vector.tensor_scalar(ve[:], mv[:, :, 1], EPS, None, ALU.add).then_inc(ln2_var, 1)

            def ln_apply(b, half):
                dve.wait_ge(ln2_rstd, b * 2 + (half + 1))
                for t in range(4):
                    ts = nc.vector.tensor_scalar(xn[:, 4 * half + t, :], xl[:, 4 * half + t, :], mv[:, t, 0:1], rs[:, t:t + 1],
                                                 ALU.subtract, ALU.mult)
                ts.then_inc(xn2_ready, 1)

            def low_x(b):
                for half in range(2):
                    for c in range(CB):
                        j = 2 * half + c
                        dve.wait_ge(x2hi_ready, b * 4 + (j + 1))
                        at = slice(half * HALF, (half + 1) * HALF)
                        tt = nc.vector.tensor_tensor(xlo[:, c, at], t2_bank[j][:], xhi[:, c, at].bitcast(F32), ALU.subtract)
                        if half == 0:
                            tt = nc.vector.tensor_tensor(xlo[:, c, T:T + P], t2_bank[j][:, 0:P], xhi[:, c, T:T + P].bitcast(F32),
                                                         ALU.subtract)
                        tt.then_inc(x2lo_ready, 1)

            def gate(b, i):
                m = i % MS
                if i >= 3:
                    dve.wait_ge(glo_ready, b * 8 + (i - 2))
                dve.wait_ge(h3_done, b * 8 + (i + 1))
                dve.wait_ge(sil_ready, b * 8 + (i + 1))
                nc.vector.scalar_tensor_tensor(gf[i % 3][:], h3_bank[i % 2][:], s3b[:, m:m + 1], sil[i % 2][:],
                                               ALU.add, ALU.mult).then_inc(gf_ready, 1)

            def low_gate(b, i):
                m, at = i % MS, slice((i // MS) * HALF, (i // MS + 1) * HALF)
                dve.wait_ge(ghi_ready, b * 8 + (i + 1))
                nc.vector.tensor_tensor(glo[:, m, at], gf[i % 3][:], ghi[:, m, at].bitcast(F32), ALU.subtract).then_inc(glo_ready, 1)

            def low_expert(b, q):
                k = expert_buffer(ORDER[q])
                dve.wait_ge(ehi_ready, b * NE + (q + 1))
                nc.vector.tensor_tensor(elo[k][:], hf[q % 2][:], ehi[k][:].bitcast(F32), ALU.subtract).then_inc(elo_ready, 1)

            def residual(b, s):
                if s == 0:
                    dve.wait_ge(biased, b + 1)
                dve.wait_ge(slot_done, b * NE + (s + 1))
                nc.vector.tensor_tensor(xr[:, s, :], o_bank[s % 2][:, 0:D], xr[:, s, :], ALU.add).then_inc(o_ready, 1)

            def batch(b, more):
                for i in range(2 * MS):
                    gate(b, i)
                    if i:
                        low_gate(b, i - 1)
                low_gate(b, 2 * MS - 1)
                low_expert(b, 0)
                low_expert(b, 1)
                for q in range(2, NE):
                    if more and q in (2, 4):
                        ln_sums(b + 1, q // 2 - 1)
                    low_expert(b, q)
                    if more and q in (2, 4):
                        ln_apply(b + 1, q // 2 - 1)
                    residual(b, q - 2)
                if more:
                    low_x(b + 1)
                residual(b, NE - 2)
                residual(b, NE - 1)

            for half in range(2):
                ln_sums(0, half)
                ln_apply(0, half)
            for n, (hi, lo, raw, scale) in enumerate(((s1hi, s1lo, s1raw, 1.0), (s3hi, s3lo, s3raw, 1.0), (r1hi, r1lo, r1raw, 1.0),
                                                      (s2hi, s2lo, s2raw, 0.5), (r2hi, r2lo, r2raw, 0.25))):
                dve.wait_ge(hi_split, n + 1)
                flat = (lambda a: a[:].rearrange("p a b -> p (a b)") if len(a.shape) == 3 else a[:].rearrange("p a b c -> p (a b c)"))
                nc.vector.scalar_tensor_tensor(flat(lo), flat(raw), scale, flat(hi).bitcast(F32), ALU.mult, ALU.subtract).then_inc(lo_split, 1)
                if n == 1:
                    low_x(0)
            dve.wait_ge(bias_landed, 32)
            nc.vector.tensor_scalar(sbias[:], sbias[:], 0.5, None, ALU.mult).then_inc(bias_part, 1)
            nc.vector.tensor_copy(bias7[:], bias[:, NE - 1, :]).then_inc(bias_part, 1)
            steps = 2
            for s in reversed(range(NE)):
                dve.wait_ge(bias_part, steps)
                before = bias[:, s - 1, :] if s else bias7[:]
                nc.vector.tensor_tensor(bias[:, s, :], bias[:, s, :], before, ALU.add).then_inc(bias_part, 1)
                steps += 1
            for s in range(NE):
                dve.wait_ge(bias_part, steps)
                bt = nc.vector.scalar_tensor_tensor(bias[:, s, :], bias[:, s, :], 0.25, sbias[:], ALU.mult, ALU.add)
            bt.then_inc(bias_ready, 1)
            with dve.Fori(0, last_batch) as b:
                batch(b, True)
            batch(last_batch, False)

        @block.gpsimd
        def _(pool):
            def passed(s, value):
                pool.wait_ge(s, value)
                pool.sem_inc(pool2_passed, 1)

            def ln_power(b, half):
                pool.wait_ge(ln2_var, b * 2 + (half + 1))
                nc.gpsimd.tensor_tensor(rs[:], ve[:], minus_half[:], ALU.pow).then_inc(ln2_rstd, 1)

            def batch(b, more):
                for i in range(2 * MS):
                    m, at = i % MS, slice((i // MS) * HALF, (i // MS + 1) * HALF)
                    passed(gf_ready, b * 8 + (i + 1))
                    nc.gpsimd.tensor_copy(ghi[:, m, at], gf[i % 3][:]).then_inc(ghi_ready, 1)
                    if i == 2 * MS - 2:
                        pool.wait_ge(xr_landed, (b + 1) * 16)
                        nc.gpsimd.tensor_tensor(xr[:], xr[:], bias[:], ALU.add).then_inc(biased, 1)
                for q in range(NE):
                    k = expert_buffer(ORDER[q])
                    passed(gelu_ready, b * NE + (q + 1))
                    nc.gpsimd.tensor_copy(ehi[k][:], hf[q % 2][:]).then_inc(ehi_ready, 1)
                    if more and q in (1, 3):
                        ln_power(b + 1, q // 2)

            nc.gpsimd.memset(minus_half[:], -0.5).then_inc(half2_set, 1)
            pool.wait_ge(half2_set, 1)
            ln_power(0, 0)
            ln_power(0, 1)
            pool.wait_ge(bias_ready, 1)
            with pool.Fori(0, last_batch) as b:
                batch(b, True)
            batch(last_batch, False)


def constants():
    import numpy as np

    residue = np.array([3 * s % NE for s in range(NE)])
    time = (np.arange(CH // NE)[None, :] * NE + residue[:, None]).reshape(-1)
    t = (np.arange(CPB)[:, None] * CH + time[None, :]).reshape(-1).astype(np.float64)
    gamma = 1.0 - 2.0 ** (-5.0 - np.arange(NH, dtype=np.float64))
    head = (np.arange(GROUPS)[None, :] * P + np.arange(P)[:, None]) // DH
    decay = np.stack([gamma[head][:, :, None] ** t * DH ** -0.5, gamma[head][:, :, None] ** -t], 1).astype(np.float32)
    masks = np.zeros((P, MASK_W), np.float32)
    own = (np.arange(P)[:, None] // DH == np.arange(P)[None, :] // DH).astype(np.float32)
    masks[:, slice(*MASK_COLS["ident"])] = np.eye(P)
    masks[:, slice(*MASK_COLS["blockmask"])] = own
    masks[:, slice(*MASK_COLS["headmean"])] = own / DH
    masks[:, slice(*MASK_COLS["causal"])] = np.tile(time[None, :] >= time[:, None], (2, 1))
    masks[:, slice(*MASK_COLS["pair"])] = (np.arange(P)[:, None] // (2 * DH)) == np.arange(PAIRS)[None, :]
    masks[:, slice(*MASK_COLS["parity"])] = (np.arange(P)[:, None] // DH % 2) == np.arange(2)[None, :]
    return decay, masks, residue


def kernel(**inputs):
    import numpy as np
    import concourse.bacc as bacc
    from concourse.bass_utils import run_bass_kernel_spmd

    f = {k: np.asarray(v) for k, v in inputs.items()}
    decay, masks, residue = constants()

    def by_partition(w):
        return w.reshape(-1, P, w.shape[-1]).transpose(1, 0, 2)

    x = f["L0_attn_x"].reshape(NBATCH, CPB, CH // NE, NE, D)[:, :, :, residue, :]
    x_chunks = x.transpose(0, 1, 3, 2, 4).reshape(NBATCH * NSUP, TILES, P, D).transpose(0, 2, 1, 3)
    x_slots = x.transpose(0, 3, 1, 2, 4).reshape(NBATCH, NE, P, D).transpose(0, 2, 1, 3).reshape(NBATCH, P, NE * D)
    arrays = {
        "xa": x_chunks,
        "xs": x_slots,
        "wattn": np.stack([by_partition(f[f"L0_attn_W_{n}"].T) for n in "qkvo"], 1),
        "gnw": f["L0_attn_gn_weight"].reshape(GROUPS, P).T,
        "gnb": f["L0_attn_gn_bias"].reshape(GROUPS, P).T,
        "sw1": by_partition(f["L0_ffn_sw1"]),
        "sw3": by_partition(f["L0_ffn_sw3"]),
        "sw2": by_partition(f["L0_ffn_sw2"]),
        "w1": f["L0_ffn_w1"].reshape(NE, CB, P, HR).transpose(2, 0, 1, 3),
        "w2": f["L0_ffn_w2"].reshape(NE, MR, P, D).transpose(2, 0, 1, 3),
        "sb1": f["L0_ffn_sb1"].reshape(MS, P).T,
        "sb3": f["L0_ffn_sb3"].reshape(MS, P).T,
        "b1": f["L0_ffn_b1"].reshape(NE, MR, P).transpose(2, 0, 1),
        "sb2": f["L0_ffn_sb2"],
        "b2": f["L0_ffn_b2"],
        "decay": decay,
        "masks": masks,
    }
    arrays = {k: np.ascontiguousarray(v) for k, v in arrays.items()}
    nc = bacc.Bacc("TRN2", target_bir_lowering=False, num_devices=1)
    args = {k: nc.dram_tensor(k, v.shape, mybir.dt.from_np(v.dtype), kind="ExternalInput").ap() for k, v in arrays.items()}
    out = nc.dram_tensor("out", [NBATCH, P, NE * D], F32, kind="ExternalOutput").ap()
    moe_retention(nc, out=out, **args)
    got = run_bass_kernel_spmd(nc, [arrays], core_ids=[0]).results[0]["out"]
    y = got.reshape(NBATCH, CPB, CH // NE, NE, D)
    return y[:, :, :, np.argsort(residue), :].reshape(NBATCH, T, D)
```

```python
from contextlib import ExitStack

import concourse.bass as bass
from concourse import mybir

F32 = mybir.dt.float32
F32R = mybir.dt.float32r
ALU = mybir.AluOpType
ACT = mybir.ActivationFunctionType

P = 128
NBATCH, T, D = 4, 1024, 256
CB = D // P
NH, DH = 16, 16
EPS = 1e-5
SUPER = 256
NSUP = T // SUPER
TILES = SUPER // P
CH = 64
CPS = SUPER // CH
CPB = T // CH
GROUPS = NH * DH // P
PAIRS = 4
NE = 8
HS, HR = 512, 256
MS, MR = HS // P, HR // P
HALF = T // 2
ORDER = [NE - 1] + list(range(NE - 1))
MASK_COLS = dict(ident=(0, P), blockmask=(P, 2 * P), headmean=(2 * P, 3 * P), causal=(3 * P, 3 * P + CH),
                  parity=(3 * P + CH, 3 * P + CH + 2))
MASK_W = 3 * P + CH + 2


def moe_retention(nc, xa, xs, wattn, gnw, gnb, sw1, sw3, sw2, w1, w2, sb1, sb3, b1, sb2, b2, decay, masks, out):
    x1_dram = nc.dram_tensor("x1_scratch", [NBATCH, P, NE * D], F32).ap()

    with ExitStack() as ctx:
        def sem(name):
            return ctx.enter_context(nc.semaphore(name))

        banks = [ctx.enter_context(nc.psum_tensor(f"bank{i}", [P, 512], F32)) for i in range(8)]
        ffn = {n: SplitWeight(nc, ctx, n, shape) for n, shape in (("sw1", [P, CB, HS]), ("sw3", [P, CB, HS]),
                                                                  ("w1", [P, NE, CB, HR]), ("sw2", [P, MS, D]))}
        phase1(nc, banks, sem, x1_dram, xa, xs, wattn, gnw, gnb, decay, masks, ffn, dict(sw1=sw1, sw3=sw3, w1=w1, sw2=sw2))
        phase2(nc, banks, sem, x1_dram, ffn, w2, sb1, sb3, b1, sb2, b2, masks, out)


class SplitWeight:

    def __init__(self, nc, ctx, name, shape):
        self.hi = ctx.enter_context(nc.sbuf_tensor(name + "_hi", shape, F32R))
        with nc.sbuf_tensor(name + "_raw", shape, F32) as self.raw:
            pass
        self.lo = ctx.enter_context(nc.sbuf_tensor(name + "_lo", shape, F32R))

    def flat(self, part):
        a = part[:]
        return a.rearrange("p a b -> p (a b)") if len(a.shape) == 3 else a.rearrange("p a b c -> p (a b c)")


def ahead(b, s, k):
    return b + (s + k) // NSUP, (s + k) % NSUP


def phase1(nc, banks, sem, x1_dram, xa, xs, wattn, gnw, gnb, decay, masks, ffn, ffn_dram):
    p_bank, s_bank, y_bank = banks[0:2], banks[2], banks[3:5]
    a_bank, b_bank, c_bank = banks[5:8]

    with ExitStack() as ctx:
        def sb(name, shape, dt=F32):
            return ctx.enter_context(nc.sbuf_tensor(name, shape, dt))

        wattn_split = SplitWeight(nc, ctx, "wattn", [P, 4, CB, D])
        whi, wlo, wraw = wattn_split.hi, wattn_split.lo, wattn_split.raw
        dec = sb("dec", [P, 2, GROUPS, T])
        msk = sb("msk", [P, MASK_W])
        gn_w = sb("gn_w", [P, GROUPS])
        gn_b = sb("gn_b", [P, GROUPS])
        minus_half = sb("minus_half", [P, 2])
        xin = [sb(f"xin{i}", [P, TILES, D]) for i in range(NSUP)]
        ln_st = sb("ln_st", [P, TILES, 6])
        ln_mv = sb("ln_mv", [P, TILES, 2])
        ln_ve = sb("ln_ve", [P, TILES])
        ln_r = sb("ln_r", [P, TILES])
        xhi = sb("xhi", [P, CB, SUPER], F32R)
        xlo = sb("xlo", [P, CB, SUPER], F32R)
        qT = [sb(f"qT{i}", [P, GROUPS, SUPER]) for i in range(2)]
        kT = [sb(f"kT{i}", [P, GROUPS, SUPER]) for i in range(2)]
        qexp = [sb(f"qexp{i}", [P, CPS, GROUPS, PAIRS, CH]) for i in range(2)]
        keo = [sb(f"keo{i}", [P, CPS, GROUPS, 2, CH]) for i in range(2)]
        ktok = [sb(f"ktok{i}", [P, TILES, GROUPS, P]) for i in range(2)]
        vtok = [sb(f"vtok{i}", [P, TILES, GROUPS, P]) for i in range(2)]
        vexp = [sb(f"vexp{i}", [P, CPS, GROUPS * PAIRS, 32]) for i in range(2)]
        pm = [sb(f"pm{i}", [P, 2 * PAIRS, CH]) for i in range(2)]
        state = [sb(f"state{i}", [P, GROUPS, P]) for i in range(2)]
        y0 = sb("y0", [P, GROUPS, SUPER])
        yT = sb("yT", [P, GROUPS, T])
        y_st = sb("y_st", [P, GROUPS, NSUP, 6])
        y_mv = sb("y_mv", [P, GROUPS, 2])
        y_mh = sb("y_mh", [P, GROUPS])
        y_d = sb("y_d", [P, GROUPS])
        y_dd = sb("y_dd", [P, GROUPS])
        y_e = sb("y_e", [P, GROUPS])
        y_ve = sb("y_ve", [P, GROUPS])
        y_r = sb("y_r", [P, GROUPS])
        y_a = sb("y_a", [P, GROUPS])
        y_ma = sb("y_ma", [P, GROUPS])
        y_b = sb("y_b", [P, GROUPS])
        yn = sb("yn", [P, GROUPS, T])
        yhi = sb("yhi", [P, GROUPS, T], F32R)
        ylo = sb("ylo", [P, GROUPS, T], F32R)
        xres = sb("xres", [P, NE, D])

        def const(name):
            return msk[:, slice(*MASK_COLS[name])]

        ident, blockmask, headmean, causal, parity = (const(n) for n in ("ident", "blockmask", "headmean", "causal", "parity"))

        x_landed = [sem(f"x_landed{i}") for i in range(NSUP)]
        w_landed = [sem(f"w{n}_landed") for n in "qkvo"]
        dec_landed, msk_landed, gn_landed = (sem(n) for n in ("dec_landed", "msk_landed", "gn_landed"))
        xres_landed, x1_stored = sem("xres_landed"), sem("x1_stored")
        whi_ready, wlo_ready, cleared, half_set = (sem(n) for n in ("whi_ready", "wlo_ready", "cleared", "half_set"))
        dve_passed, pool_passed = sem("dve_passed"), sem("pool_passed")
        ln_stats, ln_aggr, ln_var, ln_rstd, xn_ready = (sem(n) for n in ("ln_stats", "ln_aggr", "ln_var", "ln_rstd", "xn_ready"))
        t_done, xhi_ready, xlo_ready = sem("t_done"), sem("xhi_ready"), sem("xlo_ready")
        q_done, k_done, v_done, kt_done = (sem(n) for n in ("q_done", "k_done", "v_done", "kt_done"))
        keo_ready, y0_moved = sem("keo_ready"), sem("y0_moved")
        ffn_landed = {n: sem(n + "_landed") for n in ffn}
        ffn_hi, ffn_lo = sem("ffn_hi"), sem("ffn_lo")
        qT_ready, kT_ready, v_copied, ktok_copied, qexp_ready = (
            sem(n) for n in ("qT_ready", "kT_ready", "v_copied", "ktok_copied", "qexp_ready"))
        sc_done, pm_ready, y_done, y_copied, s_done, s_ready = (
            sem(n) for n in ("sc_done", "pm_ready", "y_done", "y_copied", "s_done", "s_ready"))
        y_stats, gn_aggr, gn_mean, gn_dev, gn_sq, gn_e, gn_var = (
            sem(n) for n in ("y_stats", "gn_aggr", "gn_mean", "gn_dev", "gn_sq", "gn_e", "gn_var"))
        gn_ve, gn_rstd, gn_a, gn_ma, gn_ready = (sem(n) for n in ("gn_ve", "gn_rstd", "gn_a", "gn_ma", "gn_ready"))
        yn_ready, yhi_ready, ylo_ready, o_done, x1_ready = (
            sem(n) for n in ("yn_ready", "yhi_ready", "ylo_ready", "o_done", "x1_ready"))

        block = ctx.enter_context(nc.Block())

        @block.sync
        def _(sp):
            sp.dma_start(xin[0][:], xa[0]).then_inc(x_landed[0], 16)
            sp.dma_start(msk[:], masks).then_inc(msk_landed, 16)
            for i in range(3):
                sp.dma_start(wraw[:, i], wattn[:, i]).then_inc(w_landed[i], 16)
            for s in range(1, NSUP):
                sp.dma_start(xin[s][:], xa[s]).then_inc(x_landed[s], 16)
            sp.dma_start(dec[:], decay).then_inc(dec_landed, 16)
            sp.dma_start(gn_w[:], gnw).then_inc(gn_landed, 16)
            sp.dma_start(gn_b[:], gnb).then_inc(gn_landed, 16)
            sp.dma_start(wraw[:, 3], wattn[:, 3]).then_inc(w_landed[3], 16)
            sp.dma_start(xres[:], xs[0]).then_inc(xres_landed, 16)
            for n in ffn:
                sp.dma_start(ffn[n].raw[:], ffn_dram[n]).then_inc(ffn_landed[n], 16)

            def store(b):
                sp.wait_ge(x1_ready, (b + 1) * 4)
                sp.dma_start(x1_dram[b], xres[:]).then_inc(x1_stored, 16)
                sp.wait_ge(x1_stored, (b + 1) * 16)

            def reload(b, s):
                sp.wait_ge(t_done, b * NSUP + (s + 1))
                sp.dma_start(xin[s][:], xa[b * NSUP + (NSUP + s)]).then_inc(x_landed[s], 16)

            for s in range(3):
                reload(0, s)
            with sp.Fori(0, NBATCH - 2) as b:
                reload(b, 3)
                for s in range(3):
                    reload(b + 1, s)
                store(b)
                sp.dma_start(xres[:], xs[b + 1]).then_inc(xres_landed, 16)
            reload(NBATCH - 2, 3)
            store(NBATCH - 2)
            sp.dma_start(xres[:], xs[NBATCH - 1]).then_inc(xres_landed, 16)
            store(NBATCH - 1)

        @block.tensor
        def _(pe):
            def split_product(o, w, x, first=True, last=True):
                n = len(w)
                for c in range(n):
                    for j, (l, r) in enumerate(((0, 0), (1, 0), (0, 1))):
                        mm = nc.tensor.matmul(o, w[c][l], x[c][r], start=first and c == 0 and j == 0,
                                              stop=last and c == n - 1 and j == 2)
                return mm

            def transpose_x(b, s):
                h = b * NSUP + s
                pe.wait_ge(xn_ready, h + 1)
                if not (isinstance(h, int) and h == 0):
                    pe.wait_ge(v_copied, h)
                for c in range(CB):
                    for t in range(TILES):
                        mm = nc.tensor.transpose(a_bank[:, c * SUPER + t * P:c * SUPER + (t + 1) * P],
                                                 xin[s][:, t, c * P:(c + 1) * P], ident)
                mm.then_inc(t_done, 1)

            def project(b, s):
                h = b * NSUP + s
                static0 = isinstance(h, int) and h == 0
                x = [(xhi[:, c, :], xlo[:, c, :]) for c in range(CB)]
                pe.wait_ge(xlo_ready, h + 1)
                for i, (bank, done) in enumerate(((b_bank, q_done), (c_bank, k_done))):
                    if static0:
                        pe.wait_ge(wlo_ready, i + 1)
                    elif i == 0:
                        pe.wait_ge(ktok_copied, h)
                    else:
                        pe.wait_ge(kT_ready, h)
                        if s == 2 and not (isinstance(b, int) and b == 0):
                            pe.wait_ge(gn_ve, b)
                    for g in range(GROUPS):
                        w = [(whi[:, i, c, g * P:(g + 1) * P], wlo[:, i, c, g * P:(g + 1) * P]) for c in range(CB)]
                        mm = split_product(bank[:, g * SUPER:(g + 1) * SUPER], w, x)
                    mm.then_inc(done, 1)
                if static0:
                    pe.wait_ge(wlo_ready, 3)
                for t in range(TILES):
                    w = [(xhi[:, c, t * P:(t + 1) * P], xlo[:, c, t * P:(t + 1) * P]) for c in range(CB)]
                    mm = split_product(a_bank[:, t * D:(t + 1) * D], w, [(whi[:, 2, c, :], wlo[:, 2, c, :]) for c in range(CB)])
                mm.then_inc(v_done, 1)

            def k_by_tokens(b, s):
                h = b * NSUP + s
                pe.wait_ge(kT_ready, h + 1)
                pe.wait_ge(qT_ready, h + 1)
                for t in range(TILES):
                    for g in range(GROUPS):
                        o = (t * GROUPS + g) * P
                        mm = nc.tensor.transpose(b_bank[:, o:o + P], kT[s % 2][:, g, t * P:(t + 1) * P], ident)
                mm.then_inc(kt_done, 1)

            def scores(b, s, c):
                n = (b * NSUP + s) * CPS + c
                if c == 0:
                    pe.wait_ge(keo_ready, b * NSUP + (s + 1))
                    pe.wait_ge(qexp_ready, b * NSUP + (s + 1))
                if not (isinstance(n, int) and n < 2):
                    pe.wait_ge(pm_ready, n - 1)
                for g in range(GROUPS):
                    mm = nc.tensor.matmul(p_bank[c % 2][:, g * PAIRS * CH:(g + 1) * PAIRS * CH],
                                          keo[s % 2][:, c, g, :, :], qexp[s % 2][:, c, g, :, :], start=True, stop=True)
                mm.then_inc(sc_done, 1)

            def retain(b, s, c):
                n = (b * NSUP + s) * CPS + c
                m = s * CPS + c
                if not (isinstance(n, int) and n < 2):
                    pe.wait_ge(y_copied, n - 1)
                if m > 0:
                    pe.wait_ge(s_ready, b * (CPB - 1) + m)
                    for g in range(GROUPS):
                        nc.tensor.matmul(y_bank[c % 2][:, g * CH:(g + 1) * CH], state[(c + 1) % 2][:, g, :],
                                         qT[s % 2][:, g, c * CH:(c + 1) * CH], start=(g == 0), stop=False,
                                         skip_group_check=True)
                if c == 0:
                    pe.wait_ge(v_copied, b * NSUP + (s + 1))
                pe.wait_ge(pm_ready, n + 1)
                for g in range(GROUPS):
                    for p in range(PAIRS):
                        mm = nc.tensor.matmul(y_bank[c % 2][32 * p:32 * p + 32, g * CH:(g + 1) * CH],
                                              vexp[s % 2][:, c, g * PAIRS + p, :], pm[c % 2][:, g * PAIRS + p, :],
                                              start=(m == 0 and g == 0), stop=True, skip_group_check=True)
                mm.then_inc(y_done, 1)
                if m == CPB - 1:
                    return
                if c == 0:
                    pe.wait_ge(ktok_copied, b * NSUP + (s + 1))
                t, lo = c // 2, (c % 2) * CH
                for g in range(GROUPS):
                    mm = nc.tensor.matmul(s_bank[:, g * P:(g + 1) * P], ktok[s % 2][lo:lo + CH, t, g, :],
                                          vtok[s % 2][lo:lo + CH, t, g, :], start=(m == 0 and g == 0), stop=True,
                                          skip_group_check=True)
                mm.then_inc(s_done, 1)

            def head_means(b):
                pe.wait_ge(kT_ready, (b + 1) * NSUP if isinstance(b, int) and b == NBATCH - 1 else b * NSUP + (NSUP + 2))
                pe.wait_ge(gn_aggr, b + 1)
                nc.tensor.matmul(c_bank[:, 0:GROUPS], headmean, y_mv[:, :, 0], start=True, stop=True).then_inc(gn_mean, 1)

            def head_vars(b):
                pe.wait_ge(gn_e, b + 1)
                nc.tensor.matmul(c_bank[:, 8:8 + GROUPS], headmean, y_e[:], start=True, stop=True).then_inc(gn_var, 1)

            def output(b, j, bank):
                if j == 0:
                    pe.wait_ge(ylo_ready, (b + 1) * GROUPS)
                elif bank is c_bank:
                    pe.wait_ge(x1_ready, b * 4 + j)
                for i in range(2):
                    at = (2 * j + i) * P
                    w = [(yhi[:, c, at:at + P], ylo[:, c, at:at + P]) for c in range(CB)]
                    mm = split_product(bank[:, i * D:(i + 1) * D], w, [(whi[:, 3, c, :], wlo[:, 3, c, :]) for c in range(CB)])
                mm.then_inc(o_done, 1)

            def step(b, s, norm=False, out=False):
                static = isinstance(b, int)
                g = b * NSUP + s
                more = [not (static and g + k >= NBATCH * NSUP) for k in range(3)]
                if more[1]:
                    project(*ahead(b, s, 1))
                for c in range(CPS):
                    if c == 0:
                        scores(b, s, 0)
                    if c + 1 < CPS:
                        scores(b, s, c + 1)
                    elif more[1]:
                        k_by_tokens(*ahead(b, s, 1))
                    if out and c == CPS - 1:
                        output(b - 1, c, c_bank)
                    retain(b, s, c)
                    if c == 0 and more[2]:
                        transpose_x(*ahead(b, s, 2))
                    if norm and c == 1:
                        head_means(b - 1)
                    if norm and c == 2:
                        head_vars(b - 1)
                    if out and c < CPS - 1:
                        output(b - 1, c, c_bank)
                if out:
                    pe.wait_ge(x1_ready, b * 4)

            pe.wait_ge(msk_landed, 16)
            transpose_x(0, 0)
            project(0, 0)
            transpose_x(0, 1)
            k_by_tokens(0, 0)
            step(0, 0)
            step(0, 1)
            with pe.Fori(0, NBATCH - 1) as b:
                step(b, 2)
                step(b, 3)
                step(b + 1, 0, norm=True)
                step(b + 1, 1, out=True)
            step(NBATCH - 1, 2)
            step(NBATCH - 1, 3)
            head_means(NBATCH - 1)
            head_vars(NBATCH - 1)
            for j, bank in enumerate((c_bank, b_bank, a_bank, c_bank)):
                output(NBATCH - 1, j, bank)

        @block.scalar
        def _(act):
            def high_x(b, s):
                h = b * NSUP + s
                act.wait_ge(t_done, h + 1)
                nc.scalar.activation(xhi[:].rearrange("p c t -> p (c t)"), a_bank[:], ACT.Copy).then_inc(xhi_ready, 1)

            def copy_v(b, s):
                h = b * NSUP + s
                act.wait_ge(v_done, h + 1)
                nc.scalar.activation(vtok[s % 2][:].rearrange("p t g n -> p (t g n)"), a_bank[:], ACT.Copy)
                src = a_bank[:].rearrange("p (t r h e) -> p t r h e", t=TILES, h=2, e=DH)
                dst = vexp[s % 2][:].rearrange("p (t f) r (h e) -> p t f r h e", f=2, h=2)
                for f in range(2):
                    for h2 in range(2):
                        last = nc.scalar.activation(dst[64 * h2:64 * h2 + 64, :, f, :, h2, :],
                                                    src[64 * f:64 * f + 64, :, :, h2, :], ACT.Copy)
                last.then_inc(v_copied, 1)

            def copy_k(b, s):
                h = b * NSUP + s
                act.wait_ge(kt_done, h + 1)
                nc.scalar.activation(ktok[s % 2][:].rearrange("p t g n -> p (t g n)"), b_bank[:], ACT.Copy).then_inc(ktok_copied, 1)

            def spread_q(b, s, pairs):
                h = b * NSUP + s
                if 0 in pairs:
                    act.wait_ge(qT_ready, h + 1)
                for p in pairs:
                    at = slice(32 * p, 32 * p + 32)
                    cp = nc.scalar.activation(qexp[s % 2][at, :, :, p, :], qT[s % 2][at].rearrange("p g (c i) -> p c g i", c=CPS), ACT.Copy)
                if PAIRS - 1 in pairs:
                    cp.then_inc(qexp_ready, 1)

            def copy_y(b, s, c):
                n = (b * NSUP + s) * CPS + c
                act.wait_ge(y_done, n + 1)
                if s == 0 and c == 0 and not (isinstance(b, int) and b == 0):
                    act.wait_ge(y0_moved, b)
                dst = y0[:, :, c * CH:(c + 1) * CH] if s == 0 else yT[:, :, (s * CPS + c) * CH:(s * CPS + c + 1) * CH]
                nc.scalar.activation(dst,
                                     y_bank[c % 2][:, 0:GROUPS * CH].rearrange("p (g i) -> p g i", g=GROUPS),
                                     ACT.Copy).then_inc(y_copied, 1)

            def normalise_y(b):
                act.wait_ge(gn_ready, b + 1)
                act.wait_ge(y0_moved, b + 1)
                for g in range(GROUPS):
                    nc.scalar.activation(yn[:, g, :].rearrange("p (s k u) -> p s k u", s=NE, k=CPB),
                                         yT[:, g, :].rearrange("p (k s u) -> p s k u", s=NE, k=CPB),
                                         ACT.Identity, bias=y_b[:, g:g + 1], scale=y_a[:, g:g + 1]).then_inc(yn_ready, 1)
                for g in range(GROUPS):
                    act.wait_ge(yn_ready, b * GROUPS + (g + 1))
                    nc.scalar.activation(yhi[:, g, :], yn[:, g, :], ACT.Copy).then_inc(yhi_ready, 1)

            def step(b, s, norm=False, out=False):
                static = isinstance(b, int)
                g = b * NSUP + s
                more = [not (static and g + k >= NBATCH * NSUP) for k in range(3)]
                if more[1]:
                    copy_v(*ahead(b, s, 1))
                copy_y(b, s, 0)
                if more[2]:
                    high_x(*ahead(b, s, 2))
                if more[1]:
                    spread_q(*ahead(b, s, 1), (0, 1))
                copy_y(b, s, 1)
                if more[1]:
                    spread_q(*ahead(b, s, 1), (2, 3))
                copy_y(b, s, 2)
                if more[1]:
                    copy_k(*ahead(b, s, 1))
                copy_y(b, s, 3)
                if norm:
                    normalise_y(b - 1)

            high_x(0, 0)
            for i in range(3):
                act.wait_ge(w_landed[i], 16)
                nc.scalar.activation(whi[:, i], wraw[:, i], ACT.Copy).then_inc(whi_ready, 1)
            act.wait_ge(cleared, 4)
            copy_v(0, 0)
            high_x(0, 1)
            spread_q(0, 0, range(PAIRS))
            copy_k(0, 0)
            act.wait_ge(w_landed[3], 16)
            nc.scalar.activation(whi[:, 3], wraw[:, 3], ACT.Copy).then_inc(whi_ready, 1)
            step(0, 0)
            step(0, 1)
            with act.Fori(0, NBATCH - 1) as b:
                step(b, 2)
                step(b, 3)
                step(b + 1, 0, norm=True)
                step(b + 1, 1, out=True)
            step(NBATCH - 1, 2)
            step(NBATCH - 1, 3)
            for n in ffn:
                act.wait_ge(ffn_landed[n], 16)
                nc.scalar.activation(ffn[n].hi[:], ffn[n].raw[:], ACT.Copy, scale=0.5 if n == "sw2" else 1.0).then_inc(ffn_hi, 1)
            normalise_y(NBATCH - 1)

        @block.vector
        def _(dve):
            def passed(s, value):
                dve.wait_ge(s, value)
                dve.sem_inc(dve_passed, 1)

            def ln_sums(b, s):
                h = b * NSUP + s
                dve.wait_ge(x_landed[s], (b + 1) * 16)
                for t in range(TILES):
                    st = nc.vector.bn_stats(ln_st[:, t, :], xin[s][:, t, :])
                st.then_inc(ln_stats, 1)
                passed(ln_stats, h + 1)
                for t in range(TILES):
                    ag = nc.vector.bn_aggr(ln_mv[:, t, :], ln_st[:, t, :])
                ag.then_inc(ln_aggr, 1)
                dve.wait_ge(ln_aggr, h + 1)
                nc.vector.tensor_scalar(ln_ve[:], ln_mv[:, :, 1], EPS, None, ALU.add).then_inc(ln_var, 1)

            def ln_apply(b, s):
                h = b * NSUP + s
                dve.wait_ge(ln_rstd, h + 1)
                for t in range(TILES):
                    ts = nc.vector.tensor_scalar(xin[s][:, t, :], xin[s][:, t, :], ln_mv[:, t, 0:1], ln_r[:, t:t + 1],
                                                 ALU.subtract, ALU.mult)
                ts.then_inc(xn_ready, 1)

            def spread_k(b, s, odd):
                h = b * NSUP + s
                if odd == 0:
                    dve.wait_ge(kT_ready, h + 1)
                k = kT[s % 2][:].rearrange("p g (c j) -> p c g j", c=CPS)
                ts = nc.vector.tensor_scalar(keo[s % 2][:, :, :, odd, :], k, parity[:, odd:odd + 1], None, ALU.mult)
                if odd:
                    ts.then_inc(keo_ready, 1)

            def low_x(b, s):
                h = b * NSUP + s
                dve.wait_ge(xhi_ready, h + 1)
                nc.vector.tensor_tensor(xlo[:].rearrange("p c t -> p (c t)"), a_bank[:],
                                        xhi[:].rearrange("p c t -> p (c t)").bitcast(F32), ALU.subtract).then_inc(xlo_ready, 1)

            def decay_qk(b, s, i):
                h = b * NSUP + s
                dst, bank, done, ready = ((qT, b_bank, q_done, qT_ready), (kT, c_bank, k_done, kT_ready))[i]
                dve.wait_ge(done, h + 1)
                nc.vector.tensor_tensor(dst[s % 2][:], bank[:].rearrange("p (g t) -> p g t", g=GROUPS),
                                        dec[:, i, :, s * SUPER:(s + 1) * SUPER], ALU.mult).then_inc(ready, 1)

            def mask_scores(b, s, c):
                n = (b * NSUP + s) * CPS + c
                dve.wait_ge(sc_done, n + 1)
                nc.vector.tensor_tensor(pm[c % 2][:], p_bank[c % 2][:].rearrange("p (a i) -> p a i", i=CH),
                                        causal.unsqueeze(1).broadcast_to([P, 2 * PAIRS, CH]), ALU.mult).then_inc(pm_ready, 1)

            def mask_state(b, s, c):
                m = s * CPS + c
                if m == CPB - 1:
                    return
                dve.wait_ge(s_done, b * (CPB - 1) + (m + 1))
                nc.vector.tensor_tensor(state[c % 2][:], s_bank[:, 0:GROUPS * P].rearrange("p (g e) -> p g e", g=GROUPS),
                                        blockmask.unsqueeze(1).broadcast_to([P, GROUPS, P]), ALU.mult).then_inc(s_ready, 1)

            def y_sums(b, s):
                dve.wait_ge(y_copied, (b * NSUP + (s + 1)) * CPS)
                for g in range(GROUPS):
                    st = nc.vector.bn_stats(y_st[:, g, s, :], y0[:, g, :] if s == 0 else yT[:, g, s * SUPER:(s + 1) * SUPER])
                st.then_inc(y_stats, 1)

            def gn_channels(b):
                passed(y_stats, (b + 1) * NSUP)
                for g in range(GROUPS):
                    ag = nc.vector.bn_aggr(y_mv[:, g, :], y_st[:, g, :, :].rearrange("p s k -> p (s k)"))
                ag.then_inc(gn_aggr, 1)

            def gn_spread(b):
                dve.wait_ge(gn_mean, b + 1)
                nc.vector.tensor_copy(y_mh[:], c_bank[:, 0:GROUPS])
                nc.vector.tensor_tensor(y_d[:], c_bank[:, 0:GROUPS], y_mv[:, :, 0], ALU.subtract).then_inc(gn_dev, 1)
                dve.wait_ge(gn_dev, b + 1)
                nc.vector.tensor_tensor(y_dd[:], y_d[:], y_d[:], ALU.mult).then_inc(gn_sq, 1)
                dve.wait_ge(gn_sq, b + 1)
                nc.vector.tensor_tensor(y_e[:], y_dd[:], y_mv[:, :, 1], ALU.add).then_inc(gn_e, 1)

            def gn_eps(b):
                dve.wait_ge(gn_var, b + 1)
                nc.vector.tensor_scalar(y_ve[:], c_bank[:, 8:8 + GROUPS], EPS, None, ALU.add).then_inc(gn_ve, 1)

            def gn_affine(b):
                dve.wait_ge(gn_rstd, b + 1)
                nc.vector.tensor_tensor(y_a[:], y_r[:], gn_w[:], ALU.mult).then_inc(gn_a, 1)
                dve.wait_ge(gn_a, b + 1)
                nc.vector.tensor_tensor(y_ma[:], y_mh[:], y_a[:], ALU.mult).then_inc(gn_ma, 1)
                dve.wait_ge(gn_ma, b + 1)
                nc.vector.tensor_tensor(y_b[:], gn_b[:], y_ma[:], ALU.subtract).then_inc(gn_ready, 1)

            def low_y(b):
                for g in range(GROUPS):
                    dve.wait_ge(yhi_ready, b * GROUPS + (g + 1))
                    nc.vector.tensor_tensor(ylo[:, g, :], yn[:, g, :], yhi[:, g, :].bitcast(F32), ALU.subtract).then_inc(ylo_ready, 1)

            def residual(b, j, bank):
                if j == 0:
                    dve.wait_ge(xres_landed, (b + 1) * 16)
                dve.wait_ge(o_done, b * 4 + (j + 1))
                part = xres[:, 2 * j:2 * j + 2, :].rearrange("p s d -> p (s d)")
                nc.vector.tensor_tensor(part, bank[:], part, ALU.add).then_inc(x1_ready, 1)

            def step(b, s, norm=False, out=False):
                static = isinstance(b, int)
                g = b * NSUP + s
                more = [not (static and g + k >= NBATCH * NSUP) for k in range(3)]
                if not (static and g == 0):
                    y_sums(*ahead(b - 1, s, 3))
                if norm:
                    gn_channels(b - 1)
                if more[2]:
                    ln_sums(*ahead(b, s, 2))
                if more[1]:
                    decay_qk(*ahead(b, s, 1), 0)
                    decay_qk(*ahead(b, s, 1), 1)
                if more[2]:
                    ln_apply(*ahead(b, s, 2))
                if out:
                    low_y(b - 1)
                mask_scores(b, s, 0)
                if more[1]:
                    spread_k(*ahead(b, s, 1), 0)
                mask_scores(b, s, 1)
                mask_state(b, s, 0)
                if more[2]:
                    low_x(*ahead(b, s, 2))
                if out:
                    residual(b - 1, 0, c_bank)
                mask_scores(b, s, 2)
                mask_state(b, s, 1)
                if norm:
                    gn_spread(b - 1)
                if out:
                    residual(b - 1, 1, c_bank)
                if more[1]:
                    spread_k(*ahead(b, s, 1), 1)
                mask_scores(b, s, 3)
                mask_state(b, s, 2)
                if norm:
                    gn_eps(b - 1)
                if out:
                    residual(b - 1, 2, c_bank)
                if norm:
                    gn_affine(b - 1)
                if out:
                    residual(b - 1, 3, c_bank)
                mask_state(b, s, 3)

            for i in range(2):
                nc.vector.memset(vexp[i][:], 0.0).then_inc(cleared, 1)
            ln_sums(0, 0)
            ln_apply(0, 0)
            ln_sums(0, 1)
            ln_apply(0, 1)
            low_x(0, 0)
            def low_w(i):
                dve.wait_ge(whi_ready, i + 1)
                nc.vector.tensor_tensor(wlo[:, i], wraw[:, i], whi[:, i].bitcast(F32), ALU.subtract).then_inc(wlo_ready, 1)

            for i in range(3):
                low_w(i)
            dve.wait_ge(msk_landed, 16)
            dve.wait_ge(dec_landed, 16)
            decay_qk(0, 0, 0)
            decay_qk(0, 0, 1)
            spread_k(0, 0, 0)
            spread_k(0, 0, 1)
            low_x(0, 1)
            low_w(3)
            dve.wait_ge(gn_landed, 32)
            step(0, 0)
            step(0, 1)
            with dve.Fori(0, NBATCH - 1) as b:
                step(b, 2)
                step(b, 3)
                step(b + 1, 0, norm=True)
                step(b + 1, 1, out=True)
            step(NBATCH - 1, 2)
            step(NBATCH - 1, 3)
            last = NBATCH - 1
            y_sums(last, NSUP - 1)
            gn_channels(last)
            gn_spread(last)
            gn_eps(last)
            gn_affine(last)
            low_y(last)
            for j, bank in enumerate((c_bank, b_bank, a_bank, c_bank)):
                residual(last, j, bank)

        @block.gpsimd
        def _(pool):
            def passed(s, value):
                pool.wait_ge(s, value)
                pool.sem_inc(pool_passed, 1)

            def ln_power(b, s):
                pool.wait_ge(ln_var, b * NSUP + (s + 1))
                nc.gpsimd.tensor_tensor(ln_r[:], ln_ve[:], minus_half[:], ALU.pow).then_inc(ln_rstd, 1)

            def gn_power(b):
                pool.wait_ge(gn_ve, b + 1)
                nc.gpsimd.tensor_tensor(y_r[:], y_ve[:], minus_half[:], ALU.pow).then_inc(gn_rstd, 1)

            def move_y0(b):
                if not (isinstance(b, int) and b == 0):
                    passed(yn_ready, b * GROUPS)
                passed(y_copied, b * CPB + CPS)
                nc.gpsimd.tensor_copy(yT[:, :, 0:SUPER], y0[:]).then_inc(y0_moved, 1)

            def step(b, s, norm=False, out=False):
                static = isinstance(b, int)
                g = b * NSUP + s
                if not (static and g + 2 >= NBATCH * NSUP):
                    ln_power(*ahead(b, s, 2))
                if norm:
                    gn_power(b - 1)
                if s == 1:
                    move_y0(b)

            nc.gpsimd.memset(minus_half[:], -0.5).then_inc(half_set, 1)
            pool.wait_ge(half_set, 1)
            ln_power(0, 0)
            ln_power(0, 1)
            for i in range(2):
                nc.gpsimd.memset(qexp[i][:], 0.0).then_inc(cleared, 1)
            step(0, 0)
            step(0, 1)
            with pool.Fori(0, NBATCH - 1) as b:
                step(b, 2)
                step(b, 3)
                step(b + 1, 0, norm=True)
                step(b + 1, 1, out=True)
            step(NBATCH - 1, 2)
            step(NBATCH - 1, 3)
            for i, n in enumerate(list(ffn)[:3]):
                passed(ffn_hi, i + 1)
                w = ffn[n]
                nc.gpsimd.tensor_tensor(w.flat(w.lo), w.flat(w.raw), w.flat(w.hi).bitcast(F32), ALU.subtract).then_inc(ffn_lo, 1)
            gn_power(NBATCH - 1)


def phase2(nc, banks, sem, x1_dram, ffn, w2, sb1, sb3, b1, sb2, b2, masks, out):
    h1_bank, h3_bank, e_bank, o_bank = (banks[0], banks[2]), (banks[1], banks[3]), banks[4:6], banks[6:8]
    t2_bank = banks[0:4]

    with ExitStack() as ctx:
        def sb(name, shape, dt=F32):
            return ctx.enter_context(nc.sbuf_tensor(name, shape, dt))

        w2_split = SplitWeight(nc, ctx, "w2", [P, NE, MR, D])
        s1hi, s1lo = ffn["sw1"].hi, ffn["sw1"].lo
        s3hi, s3lo = ffn["sw3"].hi, ffn["sw3"].lo
        s2hi, s2lo = ffn["sw2"].hi, ffn["sw2"].lo
        r1hi, r1lo = ffn["w1"].hi, ffn["w1"].lo
        r2hi, r2lo = w2_split.hi, w2_split.lo
        ident = sb("ident2", [P, P])
        s1b = sb("s1b", [P, MS])
        s3b = sb("s3b", [P, MS])
        r1b = sb("r1b", [P, NE, MR])
        bias = sb("bias", [P, NE, D])
        sbias = sb("sbias", [P, D])
        bias7 = sb("bias7", [P, D])
        minus_half = sb("minus_half2", [P, 4])
        xl = sb("xl", [P, NE, D])
        xr = sb("xr", [P, NE, D])
        st = sb("ln2_st", [P, 4, 6])
        mv = sb("ln2_mv", [P, 4, 2])
        ve = sb("ln2_ve", [P, 4])
        rs = sb("ln2_r", [P, 4])
        xn = sb("xn2", [P, NE, D])
        xhi = sb("x2hi", [P, CB, T + P], F32R)
        xlo = sb("x2lo", [P, CB, T + P], F32R)
        sil = [sb(f"sil{i}", [P, HALF]) for i in range(2)]
        gf = [sb(f"gf{i}", [P, HALF]) for i in range(3)]
        ghi = sb("ghi", [P, MS, T], F32R)
        glo = sb("glo", [P, MS, T], F32R)
        hf = [sb(f"hf{i}", [P, MR, 2 * P]) for i in range(2)]
        ehi = [sb(f"ehi{i}", [P, MR, 2 * P], F32R) for i in range(4)]
        elo = [sb(f"elo{i}", [P, MR, 2 * P], F32R) for i in range(4)]

        def expert_buffer(e):
            return 3 if e == NE - 1 else e % 3

        w2_landed = sem("w2_landed")
        c2_landed, bias_landed, xl_landed, xr_landed, stored = (
            sem(n) for n in ("c2_landed", "bias_landed", "xl_landed", "xr_landed", "stored"))
        hi_split, lo_split, bias_ready, bias_part, half2_set = (
            sem(n) for n in ("hi_split", "lo_split", "bias_ready", "bias_part", "half2_set"))
        dve2_passed = sem("dve2_passed")
        ln2_stats, ln2_aggr, ln2_var, ln2_rstd, xn2_ready = (
            sem(n) for n in ("ln2_stats", "ln2_aggr", "ln2_var", "ln2_rstd", "xn2_ready"))
        t2_done, x2hi_ready, x2lo_ready = sem("t2_done"), sem("x2hi_ready"), sem("x2lo_ready")
        h1_done, h3_done, sil_ready, gf_ready, ghi_ready, glo_ready = (
            sem(n) for n in ("h1_done", "h3_done", "sil_ready", "gf_ready", "ghi_ready", "glo_ready"))
        e_done, gelu_ready, ehi_ready, elo_ready, slot_done, biased, o_ready = (
            sem(n) for n in ("e_done", "gelu_ready", "ehi_ready", "elo_ready", "slot_done", "biased", "o_ready"))

        block = ctx.enter_context(nc.Block())
        last_batch = NBATCH - 1

        @block.sync
        def _(sp):
            sp.dma_start(xl[:], x1_dram[0]).then_inc(xl_landed, 16)
            sp.dma_start(ident[:], masks[:, 0:P]).then_inc(c2_landed, 16)
            for dst, src in ((s1b, sb1), (s3b, sb3), (r1b, b1)):
                sp.dma_start(dst[:], src).then_inc(c2_landed, 16)
            sp.dma_start(w2_split.raw[:], w2).then_inc(w2_landed, 16)
            sp.dma_start(xr[:], x1_dram[0]).then_inc(xr_landed, 16)
            sp.dma_start(bias[:], b2.partition_broadcast(P)).then_inc(bias_landed, 16)
            sp.dma_start(sbias[:], sb2.partition_broadcast(P)).then_inc(bias_landed, 16)

            def store(b):
                for half in range(2):
                    sp.wait_ge(o_ready, b * NE + 4 * (half + 1))
                    at = slice(4 * half, 4 * half + 4)
                    sp.dma_start(out[b].rearrange("p (s d) -> p s d", s=NE)[:, at, :], xr[:, at, :]).then_inc(stored, 16)
                sp.wait_ge(stored, (b + 1) * 32)

            with sp.Fori(0, last_batch) as b:
                sp.wait_ge(xn2_ready, (b + 1) * 2)
                sp.dma_start(xl[:], x1_dram[b + 1]).then_inc(xl_landed, 16)
                store(b)
                sp.dma_start(xr[:], x1_dram[b + 1]).then_inc(xr_landed, 16)
            store(last_batch)

        @block.tensor
        def _(pe):
            def split_product(o, w, x, first=True, last=True):
                n = len(w)
                for c in range(n):
                    for j, (l, r) in enumerate(((0, 0), (1, 0), (0, 1))):
                        mm = nc.tensor.matmul(o, w[c][l], x[c][r], start=first and c == 0 and j == 0,
                                              stop=last and c == n - 1 and j == 2)
                return mm

            def transpose_x(b):
                if not (isinstance(b, int) and b == 0):
                    pe.wait_ge(sil_ready, b * 8)
                    pe.wait_ge(gf_ready, b * 8)
                for half in range(2):
                    pe.wait_ge(xn2_ready, b * 2 + (half + 1))
                    for c in range(CB):
                        for t in range(4):
                            mm = nc.tensor.transpose(t2_bank[2 * half + c][:, t * P:(t + 1) * P],
                                                     xn[:, 4 * half + t, c * P:(c + 1) * P], ident[:])
                        mm.then_inc(t2_done, 1)

            def shared(b):
                pe.wait_ge(x2lo_ready, b * 4 + 4)
                for half in range(2):
                    x = [(xhi[:, c, half * HALF:(half + 1) * HALF], xlo[:, c, half * HALF:(half + 1) * HALF]) for c in range(CB)]
                    for m in range(MS):
                        i = half * MS + m
                        for hi, lo, bank, done, read in ((s1hi, s1lo, h1_bank, h1_done, sil_ready),
                                                         (s3hi, s3lo, h3_bank, h3_done, gf_ready)):
                            if i >= 2:
                                pe.wait_ge(read, b * 8 + (i - 1))
                            w = [(hi[:, c, m * P:(m + 1) * P], lo[:, c, m * P:(m + 1) * P]) for c in range(CB)]
                            split_product(bank[m % 2][:], w, x).then_inc(done, 1)

            def expert(b, q):
                e = ORDER[q]
                if q >= 2:
                    pe.wait_ge(gelu_ready, b * NE + (q - 1))
                x = [(xhi[:, c, e * P:(e + 2) * P], xlo[:, c, e * P:(e + 2) * P]) for c in range(CB)]
                for m in range(MR):
                    w = [(r1hi[:, e, c, m * P:(m + 1) * P], r1lo[:, e, c, m * P:(m + 1) * P]) for c in range(CB)]
                    mm = split_product(e_bank[q % 2][:, m * 2 * P:(m + 1) * 2 * P], w, x)
                mm.then_inc(e_done, 1)

            def slot(b, s):
                if s == 0 and isinstance(b, int) and b == 0:
                    pe.wait_ge(lo_split, 2)
                if s in (0, 4):
                    pe.wait_ge(glo_ready, b * 8 + (s + 4))
                if s >= 2:
                    pe.wait_ge(o_ready, b * NE + (s - 1))
                g = [(ghi[:, m, s * P:(s + 1) * P], glo[:, m, s * P:(s + 1) * P]) for m in range(MS)]
                w = [(s2hi[:, m, :], s2lo[:, m, :]) for m in range(MS)]
                if s == 0:
                    pe.wait_ge(elo_ready, b * NE + 2)
                elif s < NE - 1:
                    pe.wait_ge(elo_ready, b * NE + (s + 2))
                for e, part in (((s - 1) % NE, 1), (s, 0)):
                    k = expert_buffer(e)
                    g += [(ehi[k][:, m, part * P:(part + 1) * P], elo[k][:, m, part * P:(part + 1) * P]) for m in range(MR)]
                    w += [(r2hi[:, e, m, :], r2lo[:, e, m, :]) for m in range(MR)]
                split_product(o_bank[s % 2][:, 0:D], g, w).then_inc(slot_done, 1)

            def batch(b, more):
                shared(b)
                expert(b, 0)
                expert(b, 1)
                for q in range(2, NE):
                    expert(b, q)
                    slot(b, q - 2)
                if more:
                    transpose_x(b + 1)
                slot(b, NE - 2)
                slot(b, NE - 1)

            pe.wait_ge(c2_landed, 64)
            transpose_x(0)
            with pe.Fori(0, last_batch) as b:
                batch(b, True)
            batch(last_batch, False)

        @block.scalar
        def _(act):
            def high_x(b):
                for half in range(2):
                    for c in range(CB):
                        j = 2 * half + c
                        act.wait_ge(t2_done, b * 4 + (j + 1))
                        cp = nc.scalar.activation(xhi[:, c, half * HALF:(half + 1) * HALF], t2_bank[j][:], ACT.Copy)
                        if half == 0:
                            cp = nc.scalar.activation(xhi[:, c, T:T + P], t2_bank[j][:, 0:P], ACT.Copy)
                        cp.then_inc(x2hi_ready, 1)

            def high_gate(b, i):
                m, at = i % MS, slice((i // MS) * HALF, (i // MS + 1) * HALF)
                act.wait_ge(gf_ready, b * 8 + (i + 1))
                nc.scalar.activation(ghi[:, m, at], gf[i % 3][:], ACT.Copy).then_inc(ghi_ready, 1)

            def batch(b, more):
                for i in range(2 * MS):
                    m = i % MS
                    act.wait_ge(h1_done, b * 8 + (i + 1))
                    if i >= 2:
                        act.wait_ge(gf_ready, b * 8 + (i - 1))
                    nc.scalar.activation(sil[i % 2][:], h1_bank[i % 2][:], ACT.Silu, bias=s1b[:, m:m + 1]).then_inc(sil_ready, 1)
                    if i:
                        high_gate(b, i - 1)
                high_gate(b, 2 * MS - 1)
                for q in range(NE):
                    e = ORDER[q]
                    act.wait_ge(e_done, b * NE + (q + 1))
                    if q >= 2:
                        act.wait_ge(elo_ready, b * NE + (q - 1))
                    for m in range(MR):
                        ge = nc.scalar.activation(hf[q % 2][:, m, :], e_bank[q % 2][:, m * 2 * P:(m + 1) * 2 * P], ACT.Gelu,
                                                  bias=r1b[:, e, m:m + 1])
                    ge.then_inc(gelu_ready, 1)
                    act.wait_ge(gelu_ready, b * NE + (q + 1))
                    nc.scalar.activation(ehi[expert_buffer(e)][:], hf[q % 2][:], ACT.Copy).then_inc(ehi_ready, 1)
                if more:
                    high_x(b + 1)

            high_x(0)
            act.wait_ge(w2_landed, 16)
            nc.scalar.activation(r2hi[:], w2_split.raw[:], ACT.Copy, scale=0.25).then_inc(hi_split, 1)
            with act.Fori(0, last_batch) as b:
                batch(b, True)
            batch(last_batch, False)

        @block.vector
        def _(dve):
            def passed(s, value):
                dve.wait_ge(s, value)
                dve.sem_inc(dve2_passed, 1)

            def ln_sums(b, half):
                if half == 0:
                    dve.wait_ge(xl_landed, (b + 1) * 16)
                for t in range(4):
                    bs = nc.vector.bn_stats(st[:, t, :], xl[:, 4 * half + t, :])
                bs.then_inc(ln2_stats, 1)
                passed(ln2_stats, b * 2 + (half + 1))
                for t in range(4):
                    ag = nc.vector.bn_aggr(mv[:, t, :], st[:, t, :])
                ag.then_inc(ln2_aggr, 1)
                dve.wait_ge(ln2_aggr, b * 2 + (half + 1))
                nc.vector.tensor_scalar(ve[:], mv[:, :, 1], EPS, None, ALU.add).then_inc(ln2_var, 1)

            def ln_apply(b, half):
                dve.wait_ge(ln2_rstd, b * 2 + (half + 1))
                for t in range(4):
                    ts = nc.vector.tensor_scalar(xn[:, 4 * half + t, :], xl[:, 4 * half + t, :], mv[:, t, 0:1], rs[:, t:t + 1],
                                                 ALU.subtract, ALU.mult)
                ts.then_inc(xn2_ready, 1)

            def low_x(b):
                for half in range(2):
                    for c in range(CB):
                        j = 2 * half + c
                        dve.wait_ge(x2hi_ready, b * 4 + (j + 1))
                        at = slice(half * HALF, (half + 1) * HALF)
                        tt = nc.vector.tensor_tensor(xlo[:, c, at], t2_bank[j][:], xhi[:, c, at].bitcast(F32), ALU.subtract)
                        if half == 0:
                            tt = nc.vector.tensor_tensor(xlo[:, c, T:T + P], t2_bank[j][:, 0:P], xhi[:, c, T:T + P].bitcast(F32),
                                                         ALU.subtract)
                        tt.then_inc(x2lo_ready, 1)

            def gate(b, i):
                m = i % MS
                if i >= 3:
                    dve.wait_ge(glo_ready, b * 8 + (i - 2))
                dve.wait_ge(h3_done, b * 8 + (i + 1))
                dve.wait_ge(sil_ready, b * 8 + (i + 1))
                nc.vector.scalar_tensor_tensor(gf[i % 3][:], h3_bank[i % 2][:], s3b[:, m:m + 1], sil[i % 2][:],
                                               ALU.add, ALU.mult).then_inc(gf_ready, 1)

            def low_gate(b, i):
                m, at = i % MS, slice((i // MS) * HALF, (i // MS + 1) * HALF)
                dve.wait_ge(ghi_ready, b * 8 + (i + 1))
                nc.vector.tensor_tensor(glo[:, m, at], gf[i % 3][:], ghi[:, m, at].bitcast(F32), ALU.subtract).then_inc(glo_ready, 1)

            def low_expert(b, q):
                k = expert_buffer(ORDER[q])
                dve.wait_ge(ehi_ready, b * NE + (q + 1))
                nc.vector.tensor_tensor(elo[k][:], hf[q % 2][:], ehi[k][:].bitcast(F32), ALU.subtract).then_inc(elo_ready, 1)

            def residual(b, s):
                if s == 0:
                    dve.wait_ge(biased, b + 1)
                dve.wait_ge(slot_done, b * NE + (s + 1))
                nc.vector.tensor_tensor(xr[:, s, :], o_bank[s % 2][:, 0:D], xr[:, s, :], ALU.add).then_inc(o_ready, 1)

            def batch(b, more):
                for i in range(2 * MS):
                    gate(b, i)
                    if i:
                        low_gate(b, i - 1)
                low_gate(b, 2 * MS - 1)
                low_expert(b, 0)
                low_expert(b, 1)
                for q in range(2, NE):
                    if more and q in (2, 4):
                        ln_sums(b + 1, q // 2 - 1)
                    low_expert(b, q)
                    if more and q in (2, 4):
                        ln_apply(b + 1, q // 2 - 1)
                    residual(b, q - 2)
                if more:
                    low_x(b + 1)
                residual(b, NE - 2)
                residual(b, NE - 1)

            for half in range(2):
                ln_sums(0, half)
                ln_apply(0, half)
            low_x(0)
            sw2_split = ffn["sw2"]
            for i, (w, scale) in enumerate(((sw2_split, 0.5), (w2_split, 0.25))):
                if w is w2_split:
                    dve.wait_ge(hi_split, 1)
                nc.vector.scalar_tensor_tensor(w.flat(w.lo), w.flat(w.raw), scale, w.flat(w.hi).bitcast(F32),
                                               ALU.mult, ALU.subtract).then_inc(lo_split, 1)
            dve.wait_ge(bias_landed, 32)
            nc.vector.tensor_scalar(sbias[:], sbias[:], 0.5, None, ALU.mult).then_inc(bias_part, 1)
            nc.vector.tensor_copy(bias7[:], bias[:, NE - 1, :]).then_inc(bias_part, 1)
            steps = 2
            for s in reversed(range(NE)):
                dve.wait_ge(bias_part, steps)
                before = bias[:, s - 1, :] if s else bias7[:]
                nc.vector.tensor_tensor(bias[:, s, :], bias[:, s, :], before, ALU.add).then_inc(bias_part, 1)
                steps += 1
            for s in range(NE):
                dve.wait_ge(bias_part, steps)
                bt = nc.vector.scalar_tensor_tensor(bias[:, s, :], bias[:, s, :], 0.25, sbias[:], ALU.mult, ALU.add)
            bt.then_inc(bias_ready, 1)
            with dve.Fori(0, last_batch) as b:
                batch(b, True)
            batch(last_batch, False)

        @block.gpsimd
        def _(pool):
            def ln_power(b, half):
                pool.wait_ge(ln2_var, b * 2 + (half + 1))
                nc.gpsimd.tensor_tensor(rs[:], ve[:], minus_half[:], ALU.pow).then_inc(ln2_rstd, 1)

            def batch(b, more):
                pool.wait_ge(xr_landed, (b + 1) * 16)
                nc.gpsimd.tensor_tensor(xr[:], xr[:], bias[:], ALU.add).then_inc(biased, 1)
                if more:
                    ln_power(b + 1, 0)
                    ln_power(b + 1, 1)

            nc.gpsimd.memset(minus_half[:], -0.5).then_inc(half2_set, 1)
            pool.wait_ge(half2_set, 1)
            ln_power(0, 0)
            ln_power(0, 1)
            pool.wait_ge(bias_ready, 1)
            with pool.Fori(0, last_batch) as b:
                batch(b, True)
            batch(last_batch, False)


def constants():
    import numpy as np

    residue = np.array([3 * s % NE for s in range(NE)])
    time = (np.arange(CH // NE)[None, :] * NE + residue[:, None]).reshape(-1)
    t = (np.arange(CPB)[:, None] * CH + time[None, :]).reshape(-1).astype(np.float64)
    gamma = 1.0 - 2.0 ** (-5.0 - np.arange(NH, dtype=np.float64))
    head = (np.arange(GROUPS)[None, :] * P + np.arange(P)[:, None]) // DH
    decay = np.stack([gamma[head][:, :, None] ** t * DH ** -0.5, gamma[head][:, :, None] ** -t], 1).astype(np.float32)
    masks = np.zeros((P, MASK_W), np.float32)
    own = (np.arange(P)[:, None] // DH == np.arange(P)[None, :] // DH).astype(np.float32)
    masks[:, slice(*MASK_COLS["ident"])] = np.eye(P)
    masks[:, slice(*MASK_COLS["blockmask"])] = own
    masks[:, slice(*MASK_COLS["headmean"])] = own / DH
    masks[:, slice(*MASK_COLS["causal"])] = np.tile(time[None, :] >= time[:, None], (2, 1))
    masks[:, slice(*MASK_COLS["parity"])] = (np.arange(P)[:, None] // DH % 2) == np.arange(2)[None, :]
    return decay, masks, residue


def kernel(**inputs):
    import numpy as np
    import concourse.bacc as bacc
    from concourse.bass_utils import run_bass_kernel_spmd

    f = {k: np.asarray(v) for k, v in inputs.items()}
    decay, masks, residue = constants()

    def by_partition(w):
        return w.reshape(-1, P, w.shape[-1]).transpose(1, 0, 2)

    x = f["L0_attn_x"].reshape(NBATCH, CPB, CH // NE, NE, D)[:, :, :, residue, :]
    x_chunks = x.transpose(0, 1, 3, 2, 4).reshape(NBATCH * NSUP, TILES, P, D).transpose(0, 2, 1, 3)
    x_slots = x.transpose(0, 3, 1, 2, 4).reshape(NBATCH, NE, P, D).transpose(0, 2, 1, 3).reshape(NBATCH, P, NE * D)
    arrays = {
        "xa": x_chunks,
        "xs": x_slots,
        "wattn": np.stack([by_partition(f[f"L0_attn_W_{n}"].T) for n in "qkvo"], 1),
        "gnw": f["L0_attn_gn_weight"].reshape(GROUPS, P).T,
        "gnb": f["L0_attn_gn_bias"].reshape(GROUPS, P).T,
        "sw1": by_partition(f["L0_ffn_sw1"]),
        "sw3": by_partition(f["L0_ffn_sw3"]),
        "sw2": by_partition(f["L0_ffn_sw2"]),
        "w1": f["L0_ffn_w1"].reshape(NE, CB, P, HR).transpose(2, 0, 1, 3),
        "w2": f["L0_ffn_w2"].reshape(NE, MR, P, D).transpose(2, 0, 1, 3),
        "sb1": f["L0_ffn_sb1"].reshape(MS, P).T,
        "sb3": f["L0_ffn_sb3"].reshape(MS, P).T,
        "b1": f["L0_ffn_b1"].reshape(NE, MR, P).transpose(2, 0, 1),
        "sb2": f["L0_ffn_sb2"],
        "b2": f["L0_ffn_b2"],
        "decay": decay,
        "masks": masks,
    }
    arrays = {k: np.ascontiguousarray(v) for k, v in arrays.items()}
    nc = bacc.Bacc("TRN2", target_bir_lowering=False, num_devices=1)
    args = {k: nc.dram_tensor(k, v.shape, mybir.dt.from_np(v.dtype), kind="ExternalInput").ap() for k, v in arrays.items()}
    out = nc.dram_tensor("out", [NBATCH, P, NE * D], F32, kind="ExternalOutput").ap()
    moe_retention(nc, out=out, **args)
    got = run_bass_kernel_spmd(nc, [arrays], core_ids=[0]).results[0]["out"]
    y = got.reshape(NBATCH, CPB, CH // NE, NE, D)
    return y[:, :, :, np.argsort(residue), :].reshape(NBATCH, T, D)
```

```python
from contextlib import ExitStack

import concourse.bass as bass
from concourse import mybir

F32 = mybir.dt.float32
F32R = mybir.dt.float32r
ALU = mybir.AluOpType
ACT = mybir.ActivationFunctionType

P = 128
NBATCH, T, D = 4, 1024, 256
CB = D // P
NH, DH = 16, 16
EPS = 1e-5
SUPER = 256
NSUP = T // SUPER
TILES = SUPER // P
CH = 64
CPS = SUPER // CH
CPB = T // CH
GROUPS = NH * DH // P
PAIRS = 4
NE = 8
HS, HR = 512, 256
MS, MR = HS // P, HR // P
HALF = T // 2
WARM_UP = (5, 2)
ORDER = [NE - 1] + list(range(NE - 1))
MASK_COLS = dict(ident=(0, P), blockmask=(P, 2 * P), headmean=(2 * P, 3 * P), causal=(3 * P, 3 * P + CH),
                  parity=(3 * P + CH, 3 * P + CH + 2))
MASK_W = 3 * P + CH + 2


class SplitWeight:

    def __init__(self, nc, ctx, name, shape, lo_first=False):
        if not lo_first:
            self.hi = ctx.enter_context(nc.sbuf_tensor(name + "_hi", shape, F32R))
        with nc.sbuf_tensor(name + "_raw", shape, F32) as self.raw:
            pass
        self.lo = ctx.enter_context(nc.sbuf_tensor(name + "_lo", shape, F32R))
        if lo_first:
            self.hi = ctx.enter_context(nc.sbuf_tensor(name + "_hi", shape, F32R))

    def flat(self, part, first=0, end=None):
        a = part[:, first:end]
        return a.rearrange("p a b -> p (a b)") if len(a.shape) == 3 else a.rearrange("p a b c -> p (a b c)")


def ahead(b, s, k):
    return b + (s + k) // NSUP, (s + k) % NSUP


def moe_retention(nc, xa, xs, wattn, gnw, gnb, sw1, sw3, sw2, w1, w2, sb1, sb3, b1, sb2, b2, decay, masks, out):
    x1_dram = nc.dram_tensor("x1_scratch", [NBATCH, P, NE * D], F32).ap()
    last = NBATCH - 1

    with ExitStack() as ctx:
        def sem(name):
            return ctx.enter_context(nc.semaphore(name))

        banks = [ctx.enter_context(nc.psum_tensor(f"bank{i}", [P, 512], F32)) for i in range(8)]
        p_bank, s_bank, y_bank = banks[0:2], banks[2], banks[3:5]
        a_bank, b_bank, c_bank = banks[5:8]
        last_out_bank = (c_bank, y_bank[0], y_bank[1], s_bank)
        h1_bank, h3_bank = (a_bank, p_bank[0]), (b_bank, p_bank[1])
        t2_bank = (a_bank, b_bank, p_bank[0], p_bank[1])
        e_bank, o_bank = (*y_bank, a_bank, b_bank), (s_bank, c_bank)

        def sb(name, shape, dt=F32, stack=ctx):
            return stack.enter_context(nc.sbuf_tensor(name, shape, dt))

        sw1_split = SplitWeight(nc, ctx, "sw1", [P, CB, HS])
        sw3_split = SplitWeight(nc, ctx, "sw3", [P, CB, HS])
        wo_split = SplitWeight(nc, ctx, "wo", [P, 1, CB, D])
        msk = sb("msk", [P, MASK_W])
        gn_w = sb("gn_w", [P, GROUPS])
        gn_b = sb("gn_b", [P, GROUPS])
        minus_half = sb("minus_half", [P, 4])
        ln_st = sb("ln_st", [P, TILES, 6])
        ln_mv = sb("ln_mv", [P, TILES, 2])
        ln_ve = sb("ln_ve", [P, TILES])
        ln_r = sb("ln_r", [P, TILES])
        ln2_st = sb("ln2_st", [P, 4, 6])
        ln2_mv = sb("ln2_mv", [P, 4, 2])
        ln2_ve = sb("ln2_ve", [P, 4])
        ln2_r = sb("ln2_r", [P, 4])
        y_st = sb("y_st", [P, GROUPS, NSUP, 6])
        y_mv = sb("y_mv", [P, GROUPS, 2])
        y_mh, y_d, y_dd, y_e, y_ve, y_r, y_a, y_ma, y_b = (
            sb(n, [P, GROUPS]) for n in ("y_mh", "y_d", "y_dd", "y_e", "y_ve", "y_r", "y_a", "y_ma", "y_b"))
        s1b = sb("s1b", [P, MS])
        s3b = sb("s3b", [P, MS])
        r1b = sb("r1b", [P, NE, MR])
        slot_bias = sb("slot_bias", [P, NE, D])
        sbias = sb("sbias", [P, D])
        bias7 = sb("bias7", [P, D])
        xres = sb("xres", [P, NE, D])
        xr = sb("xr", [P, NE, D])
        hf = [xres[:, MR * i:MR * (i + 1), :] for i in range(2)]

        with ExitStack() as phase1:
            def sb_1(name, shape, dt=F32):
                return sb(name, shape, dt, phase1)

            y0 = sb_1("y0", [P, GROUPS, SUPER])
            yT = sb_1("yT", [P, GROUPS, T])
            yn = sb_1("yn", [P, GROUPS, T])
            yhi = sb_1("yhi", [P, GROUPS, T], F32R)
            ylo = sb_1("ylo", [P, GROUPS, T], F32R)
            xin = [sb_1(f"xin{i}", [P, TILES, D]) for i in range(NSUP)]
            dec = sb_1("dec", [P, 2, GROUPS, T])
            wqkv_split = SplitWeight(nc, phase1, "wqkv", [P, 3, CB, D])
            xhi = sb_1("xhi", [P, CB, SUPER], F32R)
            xlo = sb_1("xlo", [P, CB, SUPER], F32R)
            qexp_hi, qexp_lo, keo_hi, keo_lo, qT, kT, ktok, vtok, vexp = ([None, None] for _ in range(9))
            for i in range(2):
                qexp_hi[i] = sb_1(f"qexp_hi{i}", [P, CPS, GROUPS, PAIRS, CH], F32R)
                qexp_lo[i] = sb_1(f"qexp_lo{i}", [P, CPS, GROUPS, PAIRS, CH], F32R)
                keo_hi[i] = sb_1(f"keo_hi{i}", [P, CPS, GROUPS, 2, CH], F32R)
                keo_lo[i] = sb_1(f"keo_lo{i}", [P, CPS, GROUPS, 2, CH], F32R)
                qT[i] = sb_1(f"qT{i}", [P, GROUPS, SUPER])
                kT[i] = sb_1(f"kT{i}", [P, GROUPS, SUPER])
                ktok[i] = sb_1(f"ktok{i}", [P, TILES, GROUPS, P])
                vtok[i] = sb_1(f"vtok{i}", [P, TILES, GROUPS, P])
                vexp[i] = sb_1(f"vexp{i}", [P, CPS, GROUPS * PAIRS, 32])
            pm = [sb_1(f"pm{i}", [P, 2 * PAIRS, CH]) for i in range(2)]
            state = [sb_1(f"state{i}", [P, GROUPS, P]) for i in range(2)]

        gf2 = sb("gf2", [P, HALF])
        ehi = [sb(f"ehi{i}", [P, MR, 2 * P], F32R) for i in range(4)]
        elo = [sb(f"elo{i}", [P, MR, 2 * P], F32R) for i in range(4)]
        ghi1 = sb("ghi1", [P, MS, HALF], F32R)
        glo1 = sb("glo1", [P, MS, HALF], F32R)
        xl = sb("xl", [P, NE, D])
        w1_split = SplitWeight(nc, ctx, "w1", [P, NE, CB, HR], lo_first=True)
        x2hi = sb("x2hi", [P, CB, T + P], F32R)
        x2lo = sb("x2lo", [P, CB, T + P], F32R)
        sil = [sb(f"sil{i}", [P, HALF]) for i in range(2)]
        gf = [sb("gf0", [P, HALF]), sb("gf1", [P, HALF]), gf2]
        sw2_split = SplitWeight(nc, ctx, "sw2", [P, MS, D])
        w2_split = SplitWeight(nc, ctx, "w2", [P, NE, MR, D])
        ghi = [sb("ghi0", [P, MS, HALF], F32R), ghi1]
        glo = [sb("glo0", [P, MS, HALF], F32R), glo1]

        def const(name):
            return msk[:, slice(*MASK_COLS[name])]

        def by_chunks(a):
            return a[:].rearrange("p g (c j) -> p c g j", c=CPS)

        def t_bank(h):
            return p_bank[0] if isinstance(h, int) and h == 1 else a_bank

        def expert_buffer(e):
            return 3 if e == NE - 1 else e % 3

        ident, blockmask, headmean, causal, parity = (const(n) for n in ("ident", "blockmask", "headmean", "causal", "parity"))
        wo_hi, wo_lo = wo_split.hi[:, 0], wo_split.lo[:, 0]

        x_landed = [sem(f"x_landed{i}") for i in range(NSUP)]
        w_landed = [sem(f"w{n}_landed") for n in "qkvo"]
        dec0_landed, dec_landed, msk_landed, gn_landed = (sem(n) for n in ("dec0_landed", "dec_landed", "msk_landed", "gn_landed"))
        xres_landed, x1_stored = sem("xres_landed"), sem("x1_stored")
        whi_ready, wlo_ready, v_cleared, q_cleared, half_set = (
            sem(n) for n in ("whi_ready", "wlo_ready", "v_cleared", "q_cleared", "half_set"))
        dve_passed, pool_passed = sem("dve_passed"), sem("pool_passed")
        ln_stats, ln_aggr, ln_var, ln_rstd, xn_ready = (sem(n) for n in ("ln_stats", "ln_aggr", "ln_var", "ln_rstd", "xn_ready"))
        t_done, xhi_ready, xlo_ready = sem("t_done"), sem("xhi_ready"), sem("xlo_ready")
        q_done, k_done, v_done, kt_done = (sem(n) for n in ("q_done", "k_done", "v_done", "kt_done"))
        keo_hi_ready, keo_ready, y0_moved = sem("keo_hi_ready"), sem("keo_ready"), sem("y0_moved")
        sw13_landed, sw13_hi, sw13_lo = sem("sw13_landed"), sem("sw13_hi"), sem("sw13_lo")
        qT_ready, kT_ready, v_copied, ktok_copied, qexp_hi_ready, qexp_lo_ready = (
            sem(n) for n in ("qT_ready", "kT_ready", "v_copied", "ktok_copied", "qexp_hi_ready", "qexp_lo_ready"))
        sc_done, pm_ready, y_done, y_copied, s_done, s_ready = (
            sem(n) for n in ("sc_done", "pm_ready", "y_done", "y_copied", "s_done", "s_ready"))
        y_stats, gn_aggr, gn_mean, gn_dev, gn_sq, gn_e, gn_var = (
            sem(n) for n in ("y_stats", "gn_aggr", "gn_mean", "gn_dev", "gn_sq", "gn_e", "gn_var"))
        gn_ve, gn_rstd, gn_a, gn_ma, gn_ready = (sem(n) for n in ("gn_ve", "gn_rstd", "gn_a", "gn_ma", "gn_ready"))
        yn_ready, yhi_ready, ylo_ready, ylo1_ready, o_done, x1_ready = (
            sem(n) for n in ("yn_ready", "yhi_ready", "ylo_ready", "ylo1_ready", "o_done", "x1_ready"))

        w2_landed = sem("w2_landed")
        c2_landed, bias_landed, xl_landed, xr_landed, stored = (
            sem(n) for n in ("c2_landed", "bias_landed", "xl_landed", "xr_landed", "stored"))
        w1_landed, w1_hi, w1_lo = sem("w1_landed"), sem("w1_hi"), sem("w1_lo")
        sw2_landed, sw2_hi, w2_hi, w2_lo = sem("sw2_landed"), sem("sw2_hi"), sem("w2_hi"), sem("w2_lo")
        bias_ready, bias_part = sem("bias_ready"), sem("bias_part")
        ln2_stats, ln2_aggr, ln2_var, ln2_rstd, xn2_ready = (
            sem(n) for n in ("ln2_stats", "ln2_aggr", "ln2_var", "ln2_rstd", "xn2_ready"))
        t2_done, x2hi_ready, x2lo_ready = sem("t2_done"), sem("x2hi_ready"), sem("x2lo_ready")
        h1_done, h3_done, sil_ready, gf_ready, ghi_ready, glo_ready = (
            sem(n) for n in ("h1_done", "h3_done", "sil_ready", "gf_ready", "ghi_ready", "glo_ready"))
        e_done, gelu_ready, ehi_ready, elo_ready, slot_done, biased, o_ready = (
            sem(n) for n in ("e_done", "gelu_ready", "ehi_ready", "elo_ready", "slot_done", "biased", "o_ready"))

        block = ctx.enter_context(nc.Block())

        @block.sync
        def _(sp):
            sp.dma_start(xin[0][:], xa[0]).then_inc(x_landed[0], 16)
            sp.dma_start(msk[:], masks).then_inc(msk_landed, 16)
            sp.dma_start(xin[1][:], xa[1]).then_inc(x_landed[1], 16)
            sp.dma_start(dec[:, :, :, 0:SUPER], decay[:, :, :, 0:SUPER]).then_inc(dec0_landed, 16)
            for s in range(2, NSUP):
                sp.dma_start(xin[s][:], xa[s]).then_inc(x_landed[s], 16)
            sp.dma_start(dec[:, :, :, SUPER:T], decay[:, :, :, SUPER:T]).then_inc(dec_landed, 16)
            sp.dma_start(gn_w[:], gnw).then_inc(gn_landed, 16)
            sp.dma_start(gn_b[:], gnb).then_inc(gn_landed, 16)
            sp.dma_start(wo_split.raw[:, 0], wattn[:, 3]).then_inc(w_landed[3], 16)
            sp.dma_start(sw1_split.raw[:], sw1).then_inc(sw13_landed, 16)
            sp.dma_start(sw3_split.raw[:], sw3).then_inc(sw13_landed, 16)
            sp.dma_start(xres[:], xs[0]).then_inc(xres_landed, 16)
            for dst, src in ((s1b, sb1), (s3b, sb3), (r1b, b1)):
                sp.dma_start(dst[:], src).then_inc(c2_landed, 16)
            sp.dma_start(slot_bias[:], b2.partition_broadcast(P)).then_inc(bias_landed, 16)
            sp.dma_start(sbias[:], sb2.partition_broadcast(P)).then_inc(bias_landed, 16)

            def reload(b, s):
                sp.wait_ge(t_done, b * NSUP + (s + 1))
                sp.dma_start(xin[s][:], xa[b * NSUP + (NSUP + s)]).then_inc(x_landed[s], 16)

            def store_x1(b):
                sp.wait_ge(x1_ready, (b + 1) * 4)
                sp.dma_start(x1_dram[b], xres[:]).then_inc(x1_stored, 16)

            def next_xres(b):
                sp.wait_ge(x1_stored, b * 16)
                sp.dma_start(xres[:], xs[b]).then_inc(xres_landed, 16)

            def store(b):
                for half in range(2):
                    sp.wait_ge(o_ready, b * NE + 4 * (half + 1))
                    at = slice(4 * half, 4 * half + 4)
                    sp.dma_start(out[b].rearrange("p (s d) -> p s d", s=NE)[:, at, :], xr[:, at, :]).then_inc(stored, 16)
                sp.wait_ge(stored, (b + 1) * 32)

            for s in range(3):
                reload(0, s)
            with sp.Fori(0, NBATCH - 2) as b:
                reload(b, 3)
                for s in range(3):
                    reload(b + 1, s)
                store_x1(b)
                next_xres(b + 1)
            reload(NBATCH - 2, 3)
            sp.dma_start(xr[:], x1_dram[0]).then_inc(xr_landed, 16)
            sp.wait_ge(t_done, NBATCH * NSUP)
            sp.dma_start(xl[:], x1_dram[0]).then_inc(xl_landed, 16)
            store_x1(NBATCH - 2)
            sp.wait_ge(kT_ready, NBATCH * NSUP)
            sp.dma_start(w1_split.raw[:], w1).then_inc(w1_landed, 16)
            next_xres(last)
            sp.wait_ge(y_done, NBATCH * CPB)
            sp.dma_start(sw2_split.raw[:], sw2).then_inc(sw2_landed, 16)
            sp.dma_start(w2_split.raw[:], w2).then_inc(w2_landed, 16)
            store_x1(last)
            sp.wait_ge(x1_stored, NBATCH * 16)
            with sp.Fori(0, last) as b:
                sp.wait_ge(t2_done, (b + 1) * 4)
                sp.dma_start(xl[:], x1_dram[b + 1]).then_inc(xl_landed, 16)
                store(b)
                sp.dma_start(xr[:], x1_dram[b + 1]).then_inc(xr_landed, 16)
            store(last)

        @block.tensor
        def _(pe):
            def split_product(o, w, x, first=True, last=True):
                n = len(w)
                for c in range(n):
                    for j, (l, r) in enumerate(((0, 0), (1, 0), (0, 1))):
                        mm = nc.tensor.matmul(o, w[c][l], x[c][r], start=first and c == 0 and j == 0,
                                              stop=last and c == n - 1 and j == 2)
                return mm

            def transpose_x(b, s):
                h = b * NSUP + s
                bank = t_bank(h)
                pe.wait_ge(xn_ready, h + 1)
                if not (isinstance(h, int) and h <= 1):
                    pe.wait_ge(v_copied, h)
                for c in range(CB):
                    for t in range(TILES):
                        mm = nc.tensor.transpose(bank[:, c * SUPER + t * P:c * SUPER + (t + 1) * P],
                                                 xin[s][:, t, c * P:(c + 1) * P], ident)
                mm.then_inc(t_done, 1)

            def project(b, s):
                h = b * NSUP + s
                static0 = isinstance(h, int) and h == 0
                x = [(xhi[:, c, :], xlo[:, c, :]) for c in range(CB)]
                pe.wait_ge(xlo_ready, h + 1)
                for i, (bank, done) in enumerate(((b_bank, q_done), (c_bank, k_done))):
                    if static0:
                        pe.wait_ge(wlo_ready, i + 1)
                    elif i == 0:
                        pe.wait_ge(ktok_copied, h)
                    else:
                        pe.wait_ge(kT_ready, h)
                        if s == 2 and not (isinstance(b, int) and b == 0):
                            pe.wait_ge(gn_ve, b)
                    for g in range(GROUPS):
                        w = [(wqkv_split.hi[:, i, c, g * P:(g + 1) * P], wqkv_split.lo[:, i, c, g * P:(g + 1) * P]) for c in range(CB)]
                        mm = split_product(bank[:, g * SUPER:(g + 1) * SUPER], w, x)
                    mm.then_inc(done, 1)
                if static0:
                    pe.wait_ge(wlo_ready, 3)
                if isinstance(h, int) and h == 1:
                    pe.wait_ge(v_copied, 1)
                for t in range(TILES):
                    w = [(xhi[:, c, t * P:(t + 1) * P], xlo[:, c, t * P:(t + 1) * P]) for c in range(CB)]
                    mm = split_product(a_bank[:, t * D:(t + 1) * D], w, [(wqkv_split.hi[:, 2, c, :], wqkv_split.lo[:, 2, c, :]) for c in range(CB)])
                mm.then_inc(v_done, 1)

            def k_by_tokens(b, s):
                h = b * NSUP + s
                pe.wait_ge(kT_ready, h + 1)
                pe.wait_ge(qT_ready, h + 1)
                for t in range(TILES):
                    for g in range(GROUPS):
                        o = (t * GROUPS + g) * P
                        mm = nc.tensor.transpose(b_bank[:, o:o + P], kT[s % 2][:, g, t * P:(t + 1) * P], ident)
                mm.then_inc(kt_done, 1)

            def scores(b, s, c):
                n = (b * NSUP + s) * CPS + c
                if c == 0:
                    pe.wait_ge(keo_ready, b * NSUP + (s + 1))
                    pe.wait_ge(qexp_lo_ready, (b * NSUP + (s + 1)) * PAIRS)
                if not (isinstance(n, int) and n < 2):
                    pe.wait_ge(pm_ready, n - 1)
                for g in range(GROUPS):
                    mm = split_product(p_bank[c % 2][:, g * PAIRS * CH:(g + 1) * PAIRS * CH],
                                       [(keo_hi[s % 2][:, c, g, :, :], keo_lo[s % 2][:, c, g, :, :])],
                                       [(qexp_hi[s % 2][:, c, g, :, :], qexp_lo[s % 2][:, c, g, :, :])])
                mm.then_inc(sc_done, 1)

            def retain(b, s, c):
                n = (b * NSUP + s) * CPS + c
                m = s * CPS + c
                if not (isinstance(n, int) and n < 2):
                    pe.wait_ge(y_copied, n - 1)
                if m > 0:
                    pe.wait_ge(s_ready, b * (CPB - 1) + m)
                    for g in range(GROUPS):
                        nc.tensor.matmul(y_bank[c % 2][:, g * CH:(g + 1) * CH], state[(c + 1) % 2][:, g, :],
                                         qT[s % 2][:, g, c * CH:(c + 1) * CH], start=(g == 0), stop=False,
                                         skip_group_check=True)
                if c == 0:
                    pe.wait_ge(v_copied, b * NSUP + (s + 1))
                pe.wait_ge(pm_ready, n + 1)
                for g in range(GROUPS):
                    for p in range(PAIRS):
                        mm = nc.tensor.matmul(y_bank[c % 2][32 * p:32 * p + 32, g * CH:(g + 1) * CH],
                                              vexp[s % 2][:, c, g * PAIRS + p, :], pm[c % 2][:, g * PAIRS + p, :],
                                              start=(m == 0 and g == 0), stop=True, skip_group_check=True)
                mm.then_inc(y_done, 1)
                if m == CPB - 1:
                    return
                if c == 0:
                    pe.wait_ge(ktok_copied, b * NSUP + (s + 1))
                t, lo = c // 2, (c % 2) * CH
                for g in range(GROUPS):
                    mm = nc.tensor.matmul(s_bank[:, g * P:(g + 1) * P], ktok[s % 2][lo:lo + CH, t, g, :],
                                          vtok[s % 2][lo:lo + CH, t, g, :], start=(m == 0 and g == 0), stop=True,
                                          skip_group_check=True)
                mm.then_inc(s_done, 1)

            def head_means(b):
                pe.wait_ge(kT_ready, (b + 1) * NSUP if isinstance(b, int) and b == last else b * NSUP + (NSUP + 2))
                pe.wait_ge(gn_aggr, b + 1)
                nc.tensor.matmul(c_bank[:, 0:GROUPS], headmean, y_mv[:, :, 0], start=True, stop=True).then_inc(gn_mean, 1)

            def head_vars(b):
                pe.wait_ge(gn_e, b + 1)
                nc.tensor.matmul(c_bank[:, 8:8 + GROUPS], headmean, y_e[:], start=True, stop=True).then_inc(gn_var, 1)

            def output(b, j, bank):
                if j == 0:
                    if isinstance(b, int) and b == last:
                        pe.wait_ge(ylo_ready, b + GROUPS)
                    else:
                        pe.wait_ge(ylo_ready, b + 1)
                        pe.wait_ge(ylo1_ready, b + 1)
                elif not (isinstance(b, int) and b == last):
                    pe.wait_ge(x1_ready, b * 4 + j)
                for i in range(2):
                    at = (2 * j + i) * P
                    w = [(yhi[:, c, at:at + P], ylo[:, c, at:at + P]) for c in range(CB)]
                    mm = split_product(bank[:, i * D:(i + 1) * D], w, [(wo_hi[:, c, :], wo_lo[:, c, :]) for c in range(CB)])
                mm.then_inc(o_done, 1)

            def step(b, s, norm=False, out=False):
                static = isinstance(b, int)
                g = b * NSUP + s
                more = [not (static and g + k >= NBATCH * NSUP) for k in range(3)]
                if more[1]:
                    project(*ahead(b, s, 1))
                for c in range(CPS):
                    if c == 0:
                        scores(b, s, 0)
                    if c + 1 < CPS:
                        scores(b, s, c + 1)
                    elif more[1]:
                        k_by_tokens(*ahead(b, s, 1))
                    if norm and c == 2:
                        head_vars(b - 1)
                    if out and c >= 2:
                        output(b - 1, c, c_bank)
                    retain(b, s, c)
                    if c == 1 and more[2]:
                        transpose_x(*ahead(b, s, 2))
                    if norm and c == 0:
                        head_means(b - 1)
                    if out and c < 2:
                        output(b - 1, c, c_bank)
                    if c == 0 and not more[1]:
                        transpose_x2(0, 0)
                        transpose_x2(0, 1)
                if out:
                    pe.wait_ge(x1_ready, b * 4)

            def transpose_x2(b, j):
                half, c = j // CB, j % CB
                if j == 0 and not (isinstance(b, int) and b == 0):
                    pe.wait_ge(gelu_ready, b * NE)
                if c == 0:
                    pe.wait_ge(xn2_ready, b * 2 + (half + 1))
                for t in range(4):
                    mm = nc.tensor.transpose(t2_bank[j][:, t * P:(t + 1) * P],
                                             xl[:, 4 * half + t, c * P:(c + 1) * P], ident)
                mm.then_inc(t2_done, 1)

            def shared(b, i, between=None):
                half, m = i // MS, i % MS
                if i == 0:
                    pe.wait_ge(x2lo_ready, b * 4 + 2)
                elif i == 1:
                    pe.wait_ge(x2lo_ready, b * 4 + 4)
                x = [(x2hi[:, c, half * HALF:(half + 1) * HALF], x2lo[:, c, half * HALF:(half + 1) * HALF]) for c in range(CB)]
                for w13, bank, done, read in ((sw1_split, h1_bank, h1_done, sil_ready), (sw3_split, h3_bank, h3_done, gf_ready)):
                    if i >= 2:
                        pe.wait_ge(read, b * 8 + (i - 1))
                    w = [(w13.hi[:, c, m * P:(m + 1) * P], w13.lo[:, c, m * P:(m + 1) * P]) for c in range(CB)]
                    split_product(bank[m % 2][:], w, x).then_inc(done, 1)
                    if between and done is h1_done:
                        between(last)

            def expert(b, q):
                e = ORDER[q]
                if q == 2:
                    pe.wait_ge(sil_ready, b * 8 + 8)
                    pe.wait_ge(gf_ready, b * 8 + 8)
                elif q >= 4:
                    pe.wait_ge(gelu_ready, b * NE + (q - 3))
                x = [(x2hi[:, c, e * P:(e + 2) * P], x2lo[:, c, e * P:(e + 2) * P]) for c in range(CB)]
                for m in range(MR):
                    w = [(w1_split.hi[:, e, c, m * P:(m + 1) * P], w1_split.lo[:, e, c, m * P:(m + 1) * P]) for c in range(CB)]
                    mm = split_product(e_bank[q % 4][:, m * 2 * P:(m + 1) * 2 * P], w, x)
                mm.then_inc(e_done, 1)

            def slot(b, s):
                if s in (0, 4):
                    pe.wait_ge(glo_ready, b * 8 + (s + 4))
                if s >= 2:
                    pe.wait_ge(o_ready, b * NE + (s - 1))
                half, at = s // 4, slice(s % 4 * P, (s % 4 + 1) * P)
                g = [(ghi[half][:, m, at], glo[half][:, m, at]) for m in range(MS)]
                w = [(sw2_split.hi[:, m, :], sw2_split.lo[:, m, :]) for m in range(MS)]
                if s == 0:
                    pe.wait_ge(elo_ready, b * NE + 2)
                elif s < NE - 1:
                    pe.wait_ge(elo_ready, b * NE + (s + 2))
                for e, part in (((s - 1) % NE, 1), (s, 0)):
                    k = expert_buffer(e)
                    g += [(ehi[k][:, m, part * P:(part + 1) * P], elo[k][:, m, part * P:(part + 1) * P]) for m in range(MR)]
                    w += [(w2_split.hi[:, e, m, :], w2_split.lo[:, e, m, :]) for m in range(MR)]
                split_product(o_bank[s % 2][:, 0:D], g, w).then_inc(slot_done, 1)

            def experts(b, more):
                for q in range(3):
                    expert(b, q)
                for q in range(3, NE):
                    expert(b, q)
                    slot(b, q - 3)
                slot(b, NE - 3)
                if more:
                    for j in range(4):
                        transpose_x2(b + 1, j)
                slot(b, NE - 2)
                slot(b, NE - 1)

            pe.wait_ge(v_cleared, 1)
            zeros = vexp[0][:].rearrange("p c h e -> p (c h e)")

            def warm_up(n):
                for _ in range(n):
                    nc.tensor.matmul(c_bank[:, 0:2 * P], zeros[:, 0:P], zeros[:, 0:2 * P], start=True, stop=True)

            warm_up(WARM_UP[0])
            pe.wait_ge(msk_landed, 16)
            transpose_x(0, 0)
            warm_up(WARM_UP[1])
            transpose_x(0, 1)
            project(0, 0)
            k_by_tokens(0, 0)
            step(0, 0)
            step(0, 1)
            with pe.Fori(0, NBATCH - 1) as b:
                step(b, 2)
                step(b, 3)
                step(b + 1, 0, norm=True)
                step(b + 1, 1, out=True)
            step(NBATCH - 1, 2)
            step(NBATCH - 1, 3)
            transpose_x2(0, 2)
            transpose_x2(0, 3)
            pe.wait_ge(c2_landed, 48)
            pe.wait_ge(sw13_lo, 2)
            shared(0, 0, between=head_means)
            shared(0, 1, between=head_vars)
            for i in range(2, MS + 1):
                shared(0, i)
            for j in range(4):
                output(last, j, last_out_bank[j])
            for i in range(MS + 1, 2 * MS):
                shared(0, i)
            pe.wait_ge(x1_ready, NBATCH * 4)
            pe.wait_ge(w1_lo, 4)
            pe.wait_ge(w2_lo, 3)
            with pe.Fori(0, last) as b:
                experts(b, True)
                for i in range(2 * MS):
                    shared(b + 1, i)
            experts(last, False)

        @block.scalar
        def _(act):
            def high_x(b, s):
                h = b * NSUP + s
                act.wait_ge(t_done, h + 1)
                nc.scalar.activation(xhi[:].rearrange("p c t -> p (c t)"), t_bank(h)[:], ACT.Copy).then_inc(xhi_ready, 1)

            def copy_v(b, s):
                h = b * NSUP + s
                act.wait_ge(v_done, h + 1)
                nc.scalar.activation(vtok[s % 2][:].rearrange("p t g n -> p (t g n)"), a_bank[:], ACT.Copy)
                src = a_bank[:].rearrange("p (t r h e) -> p t r h e", t=TILES, h=2, e=DH)
                dst = vexp[s % 2][:].rearrange("p (t f) r (h e) -> p t f r h e", f=2, h=2)
                for f in range(2):
                    for h2 in range(2):
                        last = nc.scalar.activation(dst[64 * h2:64 * h2 + 64, :, f, :, h2, :],
                                                    src[64 * f:64 * f + 64, :, :, h2, :], ACT.Copy)
                last.then_inc(v_copied, 1)

            def copy_k(b, s):
                h = b * NSUP + s
                act.wait_ge(kt_done, h + 1)
                nc.scalar.activation(ktok[s % 2][:].rearrange("p t g n -> p (t g n)"), b_bank[:], ACT.Copy).then_inc(ktok_copied, 1)

            def spread_q(b, s):
                h = b * NSUP + s
                act.wait_ge(qT_ready, h + 1)
                for p in range(PAIRS):
                    at = slice(32 * p, 32 * p + 32)
                    cp = nc.scalar.activation(qexp_hi[s % 2][at, :, :, p, :], qT[s % 2][at].rearrange("p g (c i) -> p c g i", c=CPS),
                                              ACT.Copy)
                cp.then_inc(qexp_hi_ready, 1)

            def copy_y(b, s, c):
                n = (b * NSUP + s) * CPS + c
                act.wait_ge(y_done, n + 1)
                if s == 0 and c == 0 and not (isinstance(b, int) and b == 0):
                    act.wait_ge(y0_moved, b)
                dst = y0[:, :, c * CH:(c + 1) * CH] if s == 0 else yT[:, :, (s * CPS + c) * CH:(s * CPS + c + 1) * CH]
                nc.scalar.activation(dst,
                                     y_bank[c % 2][:, 0:GROUPS * CH].rearrange("p (g i) -> p g i", g=GROUPS),
                                     ACT.Copy).then_inc(y_copied, 1)

            def normalise_y(b):
                act.wait_ge(gn_ready, b + 1)
                act.wait_ge(y0_moved, b + 1)
                for g in range(GROUPS):
                    nc.scalar.activation(yn[:, g, :].rearrange("p (s k u) -> p s k u", s=NE, k=CPB),
                                         yT[:, g, :].rearrange("p (k s u) -> p s k u", s=NE, k=CPB),
                                         ACT.Identity, bias=y_b[:, g:g + 1], scale=y_a[:, g:g + 1]).then_inc(yn_ready, 1)

            def high_y(b, g):
                act.wait_ge(yn_ready, b * GROUPS + (g + 1))
                nc.scalar.activation(yhi[:, g, :], yn[:, g, :], ACT.Copy).then_inc(yhi_ready, 1)

            def step(b, s, norm=False, out=False):
                static = isinstance(b, int)
                g = b * NSUP + s
                more = [not (static and g + k >= NBATCH * NSUP) for k in range(3)]
                if more[1]:
                    spread_q(*ahead(b, s, 1))
                    copy_v(*ahead(b, s, 1))
                copy_y(b, s, 0)
                copy_y(b, s, 1)
                if more[2]:
                    high_x(*ahead(b, s, 2))
                copy_y(b, s, 2)
                if more[1]:
                    copy_k(*ahead(b, s, 1))
                else:
                    high_x2(0, 0)
                    high_x2(0, 1)
                copy_y(b, s, 3)
                if norm:
                    normalise_y(b - 1)
                    for g in range(GROUPS):
                        high_y(b - 1, g)

            def high_w1(part):
                if part == 0:
                    act.wait_ge(w1_landed, 16)
                es = slice(part * NE // 2, (part + 1) * NE // 2)
                nc.scalar.activation(w1_split.hi[:, es], w1_split.raw[:, es], ACT.Copy).then_inc(w1_hi, 1)

            def high_w2(part):
                if part == 0:
                    act.wait_ge(w2_landed, 16)
                es = slice(part * NE // 2, (part + 1) * NE // 2)
                nc.scalar.activation(w2_split.hi[:, es], w2_split.raw[:, es], ACT.Copy, scale=0.25).then_inc(w2_hi, 1)

            def high_x2(b, j):
                half, c = j // CB, j % CB
                act.wait_ge(t2_done, b * 4 + (j + 1))
                cp = nc.scalar.activation(x2hi[:, c, half * HALF:(half + 1) * HALF], t2_bank[j][:], ACT.Copy)
                if half == 0:
                    cp = nc.scalar.activation(x2hi[:, c, T:T + P], t2_bank[j][:, 0:P], ACT.Copy)
                cp.then_inc(x2hi_ready, 1)

            def silu(b, i):
                m = i % MS
                act.wait_ge(h1_done, b * 8 + (i + 1))
                if i >= 2:
                    act.wait_ge(gf_ready, b * 8 + (i - 1))
                nc.scalar.activation(sil[i % 2][:], h1_bank[i % 2][:], ACT.Silu, bias=s1b[:, m:m + 1]).then_inc(sil_ready, 1)

            def high_gate(b, i):
                act.wait_ge(gf_ready, b * 8 + (i + 1))
                nc.scalar.activation(ghi[i // MS][:, i % MS, :], gf[i % 3][:], ACT.Copy).then_inc(ghi_ready, 1)

            def experts(b, more):
                for q in range(NE):
                    e = ORDER[q]
                    act.wait_ge(e_done, b * NE + (q + 1))
                    if q >= 2:
                        act.wait_ge(elo_ready, b * NE + (q - 1))
                    if q >= 4:
                        act.wait_ge(slot_done, b * NE + (q - 2))
                    for m in range(MR):
                        ge = nc.scalar.activation(hf[q % 2][:, m, :], e_bank[q % 4][:, m * 2 * P:(m + 1) * 2 * P], ACT.Gelu,
                                                  bias=r1b[:, e, m:m + 1])
                    ge.then_inc(gelu_ready, 1)
                    act.wait_ge(gelu_ready, b * NE + (q + 1))
                    nc.scalar.activation(ehi[expert_buffer(e)][:], hf[q % 2][:], ACT.Copy).then_inc(ehi_ready, 1)
                    if q == 1:
                        high_gate(b, 2 * MS - 1)
                if more:
                    for j in range(4):
                        high_x2(b + 1, j)

            for i in range(3):
                act.dma_start(wqkv_split.raw[:, i], wattn[:, i]).then_inc(w_landed[i], 16)
            for i in range(3):
                act.wait_ge(w_landed[i], 16)
                nc.scalar.activation(wqkv_split.hi[:, i], wqkv_split.raw[:, i], ACT.Copy).then_inc(whi_ready, 1)
                if i == 1:
                    high_x(0, 0)
            act.wait_ge(v_cleared, 2)
            act.wait_ge(q_cleared, 4)
            spread_q(0, 0)
            act.wait_ge(v_done, 1)
            high_x(0, 1)
            copy_k(0, 0)
            copy_v(0, 0)
            act.wait_ge(w_landed[3], 16)
            nc.scalar.activation(wo_hi, wo_split.raw[:, 0], ACT.Copy).then_inc(whi_ready, 1)
            step(0, 0)
            act.wait_ge(sw13_landed, 32)
            for w in (sw1_split, sw3_split):
                nc.scalar.activation(w.hi[:], w.raw[:], ACT.Copy).then_inc(sw13_hi, 1)
            step(0, 1)
            with act.Fori(0, NBATCH - 1) as b:
                step(b, 2)
                step(b, 3)
                step(b + 1, 0, norm=True)
                step(b + 1, 1, out=True)
            step(NBATCH - 1, 2)
            step(NBATCH - 1, 3)
            high_x2(0, 2)
            high_x2(0, 3)
            silu(0, 0)
            high_w1(0)
            silu(0, 1)
            normalise_y(last)
            high_y(last, 0)
            silu(0, 2)
            high_gate(0, 0)
            high_y(last, 1)
            high_gate(0, 1)
            silu(0, 3)
            high_gate(0, 2)
            silu(0, 4)
            high_w1(1)
            high_gate(0, 3)
            act.wait_ge(sw2_landed, 16)
            nc.scalar.activation(sw2_split.hi[:], sw2_split.raw[:], ACT.Copy, scale=0.5).then_inc(sw2_hi, 1)
            high_w2(0)
            high_w2(1)
            for i in range(5, 8):
                silu(0, i)
                high_gate(0, i - 1)
            act.wait_ge(x1_stored, NBATCH * 16)
            with act.Fori(0, last) as b:
                experts(b, True)
                for i in range(2 * MS):
                    silu(b + 1, i)
                    if i:
                        high_gate(b + 1, i - 1)
            experts(last, False)

        @block.vector
        def _(dve):
            def passed(s, value):
                dve.wait_ge(s, value)
                dve.sem_inc(dve_passed, 1)

            def ln_sums(b, s):
                h = b * NSUP + s
                dve.wait_ge(x_landed[s], (b + 1) * 16)
                for t in range(TILES):
                    st = nc.vector.bn_stats(ln_st[:, t, :], xin[s][:, t, :])
                st.then_inc(ln_stats, 1)
                passed(ln_stats, h + 1)
                for t in range(TILES):
                    ag = nc.vector.bn_aggr(ln_mv[:, t, :], ln_st[:, t, :])
                ag.then_inc(ln_aggr, 1)
                dve.wait_ge(ln_aggr, h + 1)
                nc.vector.tensor_scalar(ln_ve[:], ln_mv[:, :, 1], EPS, None, ALU.add).then_inc(ln_var, 1)

            def ln_apply(b, s):
                h = b * NSUP + s
                dve.wait_ge(ln_rstd, h + 1)
                for t in range(TILES):
                    ts = nc.vector.tensor_scalar(xin[s][:, t, :], xin[s][:, t, :], ln_mv[:, t, 0:1], ln_r[:, t:t + 1],
                                                 ALU.subtract, ALU.mult)
                ts.then_inc(xn_ready, 1)

            def spread_k_hi(b, s):
                h = b * NSUP + s
                dve.wait_ge(kT_ready, h + 1)
                for odd in range(2):
                    ts = nc.vector.tensor_scalar(keo_hi[s % 2][:, :, :, odd, :], by_chunks(kT[s % 2]), parity[:, odd:odd + 1], None, ALU.mult)
                ts.then_inc(keo_hi_ready, 1)

            def spread_k_lo(b, s, odd):
                dve.wait_ge(keo_hi_ready, b * NSUP + (s + 1))
                for g in range(GROUPS):
                    tt = nc.vector.scalar_tensor_tensor(keo_lo[s % 2][:, :, g, odd, :], by_chunks(kT[s % 2])[:, :, g, :],
                                                        parity[:, odd:odd + 1], keo_hi[s % 2][:, :, g, odd, :].bitcast(F32),
                                                        ALU.mult, ALU.subtract)
                if odd:
                    tt.then_inc(keo_ready, 1)

            def low_x(b, s):
                h = b * NSUP + s
                dve.wait_ge(xhi_ready, h + 1)
                nc.vector.tensor_tensor(xlo[:].rearrange("p c t -> p (c t)"), t_bank(h)[:],
                                        xhi[:].rearrange("p c t -> p (c t)").bitcast(F32), ALU.subtract).then_inc(xlo_ready, 1)

            def decay_qk(b, s, i):
                h = b * NSUP + s
                dst, bank, done, ready = ((qT, b_bank, q_done, qT_ready), (kT, c_bank, k_done, kT_ready))[i]
                dve.wait_ge(done, h + 1)
                nc.vector.tensor_tensor(dst[s % 2][:], bank[:].rearrange("p (g t) -> p g t", g=GROUPS),
                                        dec[:, i, :, s * SUPER:(s + 1) * SUPER], ALU.mult).then_inc(ready, 1)

            def mask_scores(b, s, c):
                n = (b * NSUP + s) * CPS + c
                dve.wait_ge(sc_done, n + 1)
                nc.vector.tensor_tensor(pm[c % 2][:], p_bank[c % 2][:].rearrange("p (a i) -> p a i", i=CH),
                                        causal.unsqueeze(1).broadcast_to([P, 2 * PAIRS, CH]), ALU.mult).then_inc(pm_ready, 1)

            def mask_state(b, s, c):
                m = s * CPS + c
                if m == CPB - 1:
                    return
                dve.wait_ge(s_done, b * (CPB - 1) + (m + 1))
                nc.vector.tensor_tensor(state[c % 2][:], s_bank[:, 0:GROUPS * P].rearrange("p (g e) -> p g e", g=GROUPS),
                                        blockmask.unsqueeze(1).broadcast_to([P, GROUPS, P]), ALU.mult).then_inc(s_ready, 1)

            def y_sums(b, s):
                dve.wait_ge(y_copied, (b * NSUP + (s + 1)) * CPS)
                for g in range(GROUPS):
                    st = nc.vector.bn_stats(y_st[:, g, s, :], y0[:, g, :] if s == 0 else yT[:, g, s * SUPER:(s + 1) * SUPER])
                st.then_inc(y_stats, 1)

            def gn_channels(b):
                passed(y_stats, (b + 1) * NSUP)
                for g in range(GROUPS):
                    ag = nc.vector.bn_aggr(y_mv[:, g, :], y_st[:, g, :, :].rearrange("p s k -> p (s k)"))
                ag.then_inc(gn_aggr, 1)

            def gn_spread(b):
                dve.wait_ge(gn_mean, b + 1)
                nc.vector.tensor_copy(y_mh[:], c_bank[:, 0:GROUPS])
                nc.vector.tensor_tensor(y_d[:], c_bank[:, 0:GROUPS], y_mv[:, :, 0], ALU.subtract).then_inc(gn_dev, 1)
                dve.wait_ge(gn_dev, b + 1)
                nc.vector.tensor_tensor(y_dd[:], y_d[:], y_d[:], ALU.mult).then_inc(gn_sq, 1)
                dve.wait_ge(gn_sq, b + 1)
                nc.vector.tensor_tensor(y_e[:], y_dd[:], y_mv[:, :, 1], ALU.add).then_inc(gn_e, 1)

            def gn_eps(b):
                dve.wait_ge(gn_var, b + 1)
                nc.vector.tensor_scalar(y_ve[:], c_bank[:, 8:8 + GROUPS], EPS, None, ALU.add).then_inc(gn_ve, 1)

            def gn_affine(b):
                dve.wait_ge(gn_rstd, b + 1)
                nc.vector.tensor_tensor(y_a[:], y_r[:], gn_w[:], ALU.mult).then_inc(gn_a, 1)
                dve.wait_ge(gn_a, b + 1)
                nc.vector.tensor_tensor(y_ma[:], y_mh[:], y_a[:], ALU.mult).then_inc(gn_ma, 1)
                dve.wait_ge(gn_ma, b + 1)
                nc.vector.tensor_tensor(y_b[:], gn_b[:], y_ma[:], ALU.subtract).then_inc(gn_ready, 1)

            def low_y(b, g):
                dve.wait_ge(yhi_ready, b * GROUPS + (g + 1))
                nc.vector.tensor_tensor(ylo[:, g, :], yn[:, g, :], yhi[:, g, :].bitcast(F32), ALU.subtract).then_inc(ylo_ready, 1)

            def residual(b, j, bank):
                if j == 0:
                    dve.wait_ge(xres_landed, (b + 1) * 16)
                dve.wait_ge(o_done, b * 4 + (j + 1))
                part = xres[:, 2 * j:2 * j + 2, :].rearrange("p s d -> p (s d)")
                nc.vector.tensor_tensor(part, bank[:], part, ALU.add).then_inc(x1_ready, 1)

            def step(b, s, norm=False, out=False):
                static = isinstance(b, int)
                g = b * NSUP + s
                more = [not (static and g + k >= NBATCH * NSUP) for k in range(3)]
                early = more[1] and not more[2]
                if more[1] and not (static and g == 0):
                    y_sums(*ahead(b - 1, s, 3))
                if norm:
                    gn_channels(b - 1)
                if more[2]:
                    ln_sums(*ahead(b, s, 2))
                if early:
                    ln2_sums(0, 0)
                if more[1]:
                    decay_qk(*ahead(b, s, 1), 0)
                    decay_qk(*ahead(b, s, 1), 1)
                mask_scores(b, s, 0)
                if out:
                    low_y(b - 1, 0)
                if more[2]:
                    ln_apply(*ahead(b, s, 2))
                mask_scores(b, s, 1)
                if early:
                    ln2_apply(0, 0)
                if not more[1]:
                    y_sums(*ahead(b - 1, s, 3))
                mask_state(b, s, 0)
                if out:
                    residual(b - 1, 0, c_bank)
                mask_scores(b, s, 2)
                if more[1]:
                    spread_k_hi(*ahead(b, s, 1))
                if norm:
                    gn_spread(b - 1)
                mask_state(b, s, 1)
                if out:
                    residual(b - 1, 1, c_bank)
                mask_scores(b, s, 3)
                if norm:
                    gn_eps(b - 1)
                if out:
                    residual(b - 1, 2, c_bank)
                if more[2]:
                    low_x(*ahead(b, s, 2))
                if early:
                    spread_k_lo(*ahead(b, s, 1), 0)
                mask_state(b, s, 2)
                if more[1]:
                    spread_k_lo(*ahead(b, s, 1), 1 if early else 0)
                if norm:
                    gn_affine(b - 1)
                if out:
                    residual(b - 1, 3, c_bank)
                if not more[1]:
                    ln2_apply(0, 1)
                    low_x2(0, 0)
                    low_x2(0, 1)
                if early:
                    ln2_sums(0, 1)
                mask_state(b, s, 3)
                if more[2]:
                    spread_k_lo(*ahead(b, s, 1), 1)

            def ln2_sums(b, half):
                if half == 0:
                    dve.wait_ge(xl_landed, (b + 1) * 16)
                for t in range(4):
                    bs = nc.vector.bn_stats(ln2_st[:, t, :], xl[:, 4 * half + t, :])
                bs.then_inc(ln2_stats, 1)
                passed(ln2_stats, b * 2 + (half + 1))
                for t in range(4):
                    ag = nc.vector.bn_aggr(ln2_mv[:, t, :], ln2_st[:, t, :])
                ag.then_inc(ln2_aggr, 1)
                dve.wait_ge(ln2_aggr, b * 2 + (half + 1))
                nc.vector.tensor_scalar(ln2_ve[:], ln2_mv[:, :, 1], EPS, None, ALU.add).then_inc(ln2_var, 1)

            def ln2_apply(b, half):
                dve.wait_ge(ln2_rstd, b * 2 + (half + 1))
                for t in range(4):
                    ts = nc.vector.tensor_scalar(xl[:, 4 * half + t, :], xl[:, 4 * half + t, :], ln2_mv[:, t, 0:1], ln2_r[:, t:t + 1],
                                                 ALU.subtract, ALU.mult)
                ts.then_inc(xn2_ready, 1)

            def low_x2(b, j):
                half, c = j // CB, j % CB
                dve.wait_ge(x2hi_ready, b * 4 + (j + 1))
                at = slice(half * HALF, (half + 1) * HALF)
                tt = nc.vector.tensor_tensor(x2lo[:, c, at], t2_bank[j][:], x2hi[:, c, at].bitcast(F32), ALU.subtract)
                if half == 0:
                    tt = nc.vector.tensor_tensor(x2lo[:, c, T:T + P], t2_bank[j][:, 0:P], x2hi[:, c, T:T + P].bitcast(F32),
                                                 ALU.subtract)
                tt.then_inc(x2lo_ready, 1)

            def gate(b, i):
                m = i % MS
                if i >= 3:
                    dve.wait_ge(glo_ready, b * 8 + (i - 2))
                dve.wait_ge(h3_done, b * 8 + (i + 1))
                dve.wait_ge(sil_ready, b * 8 + (i + 1))
                nc.vector.scalar_tensor_tensor(gf[i % 3][:], h3_bank[i % 2][:], s3b[:, m:m + 1], sil[i % 2][:],
                                               ALU.add, ALU.mult).then_inc(gf_ready, 1)

            def low_gate(b, i):
                half, m = i // MS, i % MS
                dve.wait_ge(ghi_ready, b * 8 + (i + 1))
                nc.vector.tensor_tensor(glo[half][:, m, :], gf[i % 3][:], ghi[half][:, m, :].bitcast(F32),
                                        ALU.subtract).then_inc(glo_ready, 1)

            def low_expert(b, q):
                k = expert_buffer(ORDER[q])
                dve.wait_ge(ehi_ready, b * NE + (q + 1))
                nc.vector.tensor_tensor(elo[k][:], hf[q % 2][:], ehi[k][:].bitcast(F32), ALU.subtract).then_inc(elo_ready, 1)

            def add_slot(b, s):
                if s == 0:
                    dve.wait_ge(biased, b + 1)
                dve.wait_ge(slot_done, b * NE + (s + 1))
                nc.vector.tensor_tensor(xr[:, s, :], o_bank[s % 2][:, 0:D], xr[:, s, :], ALU.add).then_inc(o_ready, 1)

            def experts(b, more):
                low_expert(b, 0)
                low_expert(b, 1)
                low_gate(b, 2 * MS - 1)
                for q in range(2, NE):
                    if more and q in (2, 4):
                        ln2_sums(b + 1, q // 2 - 1)
                    low_expert(b, q)
                    if more and q in (2, 4):
                        ln2_apply(b + 1, q // 2 - 1)
                    add_slot(b, q - 2)
                if more:
                    for j in range(4):
                        low_x2(b + 1, j)
                add_slot(b, NE - 2)
                add_slot(b, NE - 1)

            def slot_bias_means():
                dve.wait_ge(bias_part, NE + 1)
                for s in range(NE):
                    bt = nc.vector.scalar_tensor_tensor(slot_bias[:, s, :], slot_bias[:, s, :], 0.25, sbias[:], ALU.mult, ALU.add)
                bt.then_inc(bias_ready, 1)

            def low_w2(w, hi_done, scale, first, end):
                dve.wait_ge(*hi_done)
                nc.vector.scalar_tensor_tensor(w.flat(w.lo, first, end), w.flat(w.raw, first, end), scale,
                                               w.flat(w.hi, first, end).bitcast(F32), ALU.mult, ALU.subtract).then_inc(w2_lo, 1)

            for i in range(2):
                nc.vector.memset(vexp[i][:], 0.0).then_inc(v_cleared, 1)
            ln_sums(0, 0)
            ln_apply(0, 0)
            ln_sums(0, 1)

            def low_w(i):
                w, j = (wqkv_split, i) if i < 3 else (wo_split, 0)
                lo, raw, hi = w.lo[:, j], w.raw[:, j], w.hi[:, j]
                dve.wait_ge(whi_ready, i + 1)
                nc.vector.tensor_tensor(lo, raw, hi.bitcast(F32), ALU.subtract).then_inc(wlo_ready, 1)

            low_w(0)
            ln_apply(0, 1)
            low_x(0, 0)
            low_w(1)
            low_w(2)
            dve.wait_ge(msk_landed, 16)
            dve.wait_ge(dec0_landed, 16)
            decay_qk(0, 0, 0)
            decay_qk(0, 0, 1)
            low_x(0, 1)
            spread_k_hi(0, 0)
            spread_k_lo(0, 0, 0)
            spread_k_lo(0, 0, 1)
            low_w(3)
            dve.wait_ge(gn_landed, 32)
            dve.wait_ge(dec_landed, 16)
            step(0, 0)
            step(0, 1)
            with dve.Fori(0, NBATCH - 1) as b:
                step(b, 2)
                step(b, 3)
                step(b + 1, 0, norm=True)
                step(b + 1, 1, out=True)
            step(NBATCH - 1, 2)
            step(NBATCH - 1, 3)
            y_sums(last, NSUP - 1)
            gn_channels(last)
            low_x2(0, 2)
            low_x2(0, 3)
            gn_spread(last)
            gn_eps(last)
            gate(0, 0)
            gn_affine(last)
            gate(0, 1)
            slot_bias_means()
            low_y(last, 0)
            gate(0, 2)
            low_gate(0, 0)
            low_y(last, 1)
            low_gate(0, 1)
            gate(0, 3)
            low_gate(0, 2)
            low_gate(0, 3)
            gate(0, 4)
            low_w2(sw2_split, (sw2_hi, 1), 0.5, 0, MS)
            residual(last, 0, last_out_bank[0])
            residual(last, 1, last_out_bank[1])
            low_w2(w2_split, (w2_hi, 1), 0.25, 0, NE // 2)
            residual(last, 2, last_out_bank[2])
            residual(last, 3, last_out_bank[3])
            low_w2(w2_split, (w2_hi, 2), 0.25, NE // 2, NE)
            for i in range(5, 8):
                gate(0, i)
                low_gate(0, i - 1)
            with dve.Fori(0, last) as b:
                experts(b, True)
                for i in range(2 * MS):
                    gate(b + 1, i)
                    if i:
                        low_gate(b + 1, i - 1)
            experts(last, False)

        @block.gpsimd
        def _(pool):
            def passed(s, value):
                pool.wait_ge(s, value)
                pool.sem_inc(pool_passed, 1)

            def ln_power(b, s):
                pool.wait_ge(ln_var, b * NSUP + (s + 1))
                nc.gpsimd.tensor_tensor(ln_r[:], ln_ve[:], minus_half[:, 0:TILES], ALU.pow).then_inc(ln_rstd, 1)

            def gn_power(b):
                pool.wait_ge(gn_ve, b + 1)
                nc.gpsimd.tensor_tensor(y_r[:], y_ve[:], minus_half[:, 0:GROUPS], ALU.pow).then_inc(gn_rstd, 1)

            def move_y0(b):
                if not (isinstance(b, int) and b == 0):
                    passed(yn_ready, b * GROUPS)
                passed(y_copied, b * CPB + CPS)
                nc.gpsimd.tensor_copy(yT[:, :, 0:SUPER], y0[:]).then_inc(y0_moved, 1)

            def low_y(b):
                passed(yhi_ready, (b + 1) * GROUPS)
                nc.gpsimd.tensor_tensor(ylo[:, 1, :], yn[:, 1, :], yhi[:, 1, :].bitcast(F32), ALU.subtract).then_inc(ylo1_ready, 1)

            def spread_q_low(b, s):
                h = b * NSUP + s
                passed(qexp_hi_ready, h + 1)
                for p in range(PAIRS):
                    if p:
                        pool.wait_ge(qexp_lo_ready, h * PAIRS + p)
                    at = slice(32 * p, 32 * p + 32)
                    nc.gpsimd.tensor_tensor(qexp_lo[s % 2][at, :, :, p, :], by_chunks(qT[s % 2])[at],
                                            qexp_hi[s % 2][at, :, :, p, :].bitcast(F32), ALU.subtract).then_inc(qexp_lo_ready, 1)
                passed(qexp_lo_ready, (h + 1) * PAIRS)

            def step(b, s, norm=False, out=False):
                static = isinstance(b, int)
                g = b * NSUP + s
                if not (static and g + 2 >= NBATCH * NSUP):
                    ln_power(*ahead(b, s, 2))
                if out:
                    low_y(b - 1)
                if static and g + 2 == NBATCH * NSUP:
                    ln2_power(0, 0)
                if not (static and g + 1 >= NBATCH * NSUP):
                    spread_q_low(*ahead(b, s, 1))
                if norm:
                    gn_power(b - 1)
                if s == 1:
                    move_y0(b)

            def ln2_power(b, half):
                pool.wait_ge(ln2_var, b * 2 + (half + 1))
                nc.gpsimd.tensor_tensor(ln2_r[:], ln2_ve[:], minus_half[:], ALU.pow).then_inc(ln2_rstd, 1)

            def experts(b, more):
                pool.wait_ge(xr_landed, (b + 1) * 16)
                nc.gpsimd.tensor_tensor(xr[:], xr[:], slot_bias[:], ALU.add).then_inc(biased, 1)
                if more:
                    ln2_power(b + 1, 0)
                    ln2_power(b + 1, 1)

            def low_w(w, hi_ready, count, first, end, done):
                passed(hi_ready, count)
                nc.gpsimd.tensor_tensor(w.flat(w.lo, first, end), w.flat(w.raw, first, end),
                                        w.flat(w.hi, first, end).bitcast(F32), ALU.subtract).then_inc(done, 1)

            def slot_bias_sums():
                pool.wait_ge(bias_landed, 32)
                nc.gpsimd.tensor_scalar(sbias[:], sbias[:], 0.5, None, ALU.mult)
                nc.gpsimd.tensor_copy(bias7[:], slot_bias[:, NE - 1, :]).then_inc(bias_part, 1)
                for i, s in enumerate(reversed(range(NE))):
                    pool.wait_ge(bias_part, i + 1)
                    before = slot_bias[:, s - 1, :] if s else bias7[:]
                    nc.gpsimd.tensor_tensor(slot_bias[:, s, :], slot_bias[:, s, :], before, ALU.add).then_inc(bias_part, 1)

            nc.gpsimd.memset(minus_half[:], -0.5).then_inc(half_set, 1)
            pool.wait_ge(half_set, 1)
            def clear_q(i):
                for q in (qexp_hi[i], qexp_lo[i]):
                    nc.gpsimd.memset(q[:].bitcast(F32), 0.0).then_inc(q_cleared, 1)

            clear_q(0)
            ln_power(0, 0)
            ln_power(0, 1)
            clear_q(1)
            spread_q_low(0, 0)
            step(0, 0)
            step(0, 1)
            for i, w in enumerate((sw1_split, sw3_split)):
                low_w(w, sw13_hi, i + 1, 0, CB, sw13_lo)
            with pool.Fori(0, NBATCH - 1) as b:
                step(b, 2)
                step(b, 3)
                step(b + 1, 0, norm=True)
                step(b + 1, 1, out=True)
            step(NBATCH - 1, 2)
            step(NBATCH - 1, 3)
            ln2_power(0, 1)
            slot_bias_sums()
            gn_power(last)
            for part in range(4):
                low_w(w1_split, w1_hi, part // 2 + 1, part * NE // 4, (part + 1) * NE // 4, w1_lo)
            pool.wait_ge(bias_ready, 1)
            with pool.Fori(0, last) as b:
                experts(b, True)
            experts(last, False)


def constants():
    import numpy as np

    residue = np.array([3 * s % NE for s in range(NE)])
    time = (np.arange(CH // NE)[None, :] * NE + residue[:, None]).reshape(-1)
    t = (np.arange(CPB)[:, None] * CH + time[None, :]).reshape(-1).astype(np.float64)
    gamma = 1.0 - 2.0 ** (-5.0 - np.arange(NH, dtype=np.float64))
    head = (np.arange(GROUPS)[None, :] * P + np.arange(P)[:, None]) // DH
    decay = np.stack([gamma[head][:, :, None] ** t * DH ** -0.5, gamma[head][:, :, None] ** -t], 1).astype(np.float32)
    masks = np.zeros((P, MASK_W), np.float32)
    own = (np.arange(P)[:, None] // DH == np.arange(P)[None, :] // DH).astype(np.float32)
    masks[:, slice(*MASK_COLS["ident"])] = np.eye(P)
    masks[:, slice(*MASK_COLS["blockmask"])] = own
    masks[:, slice(*MASK_COLS["headmean"])] = own / DH
    masks[:, slice(*MASK_COLS["causal"])] = np.tile(time[None, :] >= time[:, None], (2, 1))
    masks[:, slice(*MASK_COLS["parity"])] = (np.arange(P)[:, None] // DH % 2) == np.arange(2)[None, :]
    return decay, masks, residue


def kernel(**inputs):
    import numpy as np
    import concourse.bacc as bacc
    from concourse.bass_utils import run_bass_kernel_spmd

    f = {k: np.asarray(v) for k, v in inputs.items()}
    decay, masks, residue = constants()

    def by_partition(w):
        return w.reshape(-1, P, w.shape[-1]).transpose(1, 0, 2)

    x = f["L0_attn_x"].reshape(NBATCH, CPB, CH // NE, NE, D)[:, :, :, residue, :]
    x_chunks = x.transpose(0, 1, 3, 2, 4).reshape(NBATCH * NSUP, TILES, P, D).transpose(0, 2, 1, 3)
    x_slots = x.transpose(0, 3, 1, 2, 4).reshape(NBATCH, NE, P, D).transpose(0, 2, 1, 3).reshape(NBATCH, P, NE * D)
    arrays = {
        "xa": x_chunks,
        "xs": x_slots,
        "wattn": np.stack([by_partition(f[f"L0_attn_W_{n}"].T) for n in "qkvo"], 1),
        "gnw": f["L0_attn_gn_weight"].reshape(GROUPS, P).T,
        "gnb": f["L0_attn_gn_bias"].reshape(GROUPS, P).T,
        "sw1": by_partition(f["L0_ffn_sw1"]),
        "sw3": by_partition(f["L0_ffn_sw3"]),
        "sw2": by_partition(f["L0_ffn_sw2"]),
        "w1": f["L0_ffn_w1"].reshape(NE, CB, P, HR).transpose(2, 0, 1, 3),
        "w2": f["L0_ffn_w2"].reshape(NE, MR, P, D).transpose(2, 0, 1, 3),
        "sb1": f["L0_ffn_sb1"].reshape(MS, P).T,
        "sb3": f["L0_ffn_sb3"].reshape(MS, P).T,
        "b1": f["L0_ffn_b1"].reshape(NE, MR, P).transpose(2, 0, 1),
        "sb2": f["L0_ffn_sb2"],
        "b2": f["L0_ffn_b2"],
        "decay": decay,
        "masks": masks,
    }
    arrays = {k: np.ascontiguousarray(v) for k, v in arrays.items()}
    nc = bacc.Bacc("TRN2", target_bir_lowering=False, num_devices=1)
    args = {k: nc.dram_tensor(k, v.shape, mybir.dt.from_np(v.dtype), kind="ExternalInput").ap() for k, v in arrays.items()}
    out = nc.dram_tensor("out", [NBATCH, P, NE * D], F32, kind="ExternalOutput").ap()
    moe_retention(nc, out=out, **args)
    got = run_bass_kernel_spmd(nc, [arrays], core_ids=[0]).results[0]["out"]
    y = got.reshape(NBATCH, CPB, CH // NE, NE, D)
    return y[:, :, :, np.argsort(residue), :].reshape(NBATCH, T, D)
```
